# Optimizing a Trainium2 kernel written in Bass

```python
import numpy as np
import jax
import jax.numpy as jnp

def _softmax(x, axis=-1):
    return jax.nn.softmax(x, axis=axis)

def _gelu(x):
    return jax.nn.gelu(x, approximate=True)

def _silu(x):
    return jax.nn.silu(x)

def _sigmoid(x):
    return jax.nn.sigmoid(x)

def _layernorm(x, axis=-1, eps=1e-05):
    m = jnp.mean(x, axis=axis, keepdims=True)
    v = jnp.var(x, axis=axis, keepdims=True)
    return (x - m) / jnp.sqrt(v + eps)

def _scatter_add(tgt, idx, src, axis=0):
    return tgt.at[idx].add(src)

def _segment_sum(src, seg, n):
    return jax.ops.segment_sum(src, seg, n)
kernel_name = 'mk_macaron_d1_jaxref_r8_a82a2f'

def setup_inputs(seed: int=0):
    np.random.seed(seed)
    _w = jnp.asarray

    def _L0_attn_setup():
        import jax, jax.numpy as jnp
        import numpy as np
        DECAY = 0.95

        def smear(x, decay):
            a = jnp.full_like(x, decay)

            def combine(c1, c2):
                a1, b1 = c1
                a2, b2 = c2
                return (a1 * a2, a2 * b1 + b2)
            _, y = jax.lax.associative_scan(combine, (a, x), axis=1)
            return y
        key = jax.random.key(seed)
        ks = jax.random.split(key, 5)
        B, S, E, M = (4, 512, 256, 256)
        x = jax.random.normal(ks[0], (B, S, E), dtype=jnp.float32)
        s = 0.02
        Wv = jax.random.normal(ks[1], (E, M), dtype=jnp.float32) * s
        Wg = jax.random.normal(ks[2], (E, M), dtype=jnp.float32) * s
        bg = jnp.zeros((M,), dtype=jnp.float32)
        Wq = jax.random.normal(ks[3], (E, M), dtype=jnp.float32) * s
        bq = jnp.zeros((M,), dtype=jnp.float32)
        Wo = jax.random.normal(ks[4], (M, E), dtype=jnp.float32) * s
        return {'x': x, 'Wv': Wv, 'Wg': Wg, 'bg': bg, 'Wq': Wq, 'bq': bq, 'Wo': Wo}
    _L0_attn_in = _L0_attn_setup()

    def _L0_ffn_setup():
        import jax, jax.numpy as jnp
        import numpy as np
        B, S, D_IN, D_OUT, E = (4, 128, 256, 256, 32)
        MASK_DENSITY = 0.3
        THRESH = 0.5
        key = jax.random.key(seed)
        k_x, k_w, k_m, k_r = jax.random.split(key, 4)
        x = jax.random.normal(k_x, (B, S, D_IN), dtype=jnp.float32)
        bound = np.sqrt(1.0 / D_IN) * np.sqrt(3.0)
        weight = jax.random.uniform(k_w, (D_OUT, D_IN), minval=-bound, maxval=bound, dtype=jnp.float32)
        scale = jnp.ones((D_OUT,), dtype=jnp.float32)
        expert_masks = (jax.random.uniform(k_m, (E, D_OUT, D_IN)) < MASK_DENSITY).astype(jnp.float32)
        router_w = 0.01 * jax.random.normal(k_r, (E, D_IN), dtype=jnp.float32)
        return {'x': x, 'weight': weight, 'scale': scale, 'expert_masks': expert_masks, 'router_w': router_w}
    _L0_ffn_in = _L0_ffn_setup()
    _d = {'L0_attn_x': _L0_attn_in['x'], 'L0_attn_Wv': _L0_attn_in['Wv'], 'L0_attn_Wg': _L0_attn_in['Wg'], 'L0_attn_bg': _L0_attn_in['bg'], 'L0_attn_Wq': _L0_attn_in['Wq'], 'L0_attn_bq': _L0_attn_in['bq'], 'L0_attn_Wo': _L0_attn_in['Wo'], 'L0_ffn_weight': _L0_ffn_in['weight'], 'L0_ffn_scale': _L0_ffn_in['scale'], 'L0_ffn_expert_masks': _L0_ffn_in['expert_masks'], 'L0_ffn_router_w': _L0_ffn_in['router_w']}
    _x0 = _d['L0_attn_x']
    _d['L0_attn_x'] = jax.random.normal(jax.random.fold_in(jax.random.key(seed), 1), (8, 256, 256), dtype=_x0.dtype)
    del _x0
    return _d

def reference(L0_attn_x, L0_attn_Wv, L0_attn_Wg, L0_attn_bg, L0_attn_Wq, L0_attn_bq, L0_attn_Wo, L0_ffn_weight, L0_ffn_scale, L0_ffn_expert_masks, L0_ffn_router_w):

    def _L0_attn_ref(x, Wv, Wg, bg, Wq, bq, Wo):
        import jax, jax.numpy as jnp
        import numpy as np
        DECAY = 0.95

        def smear(x, decay):
            a = jnp.full_like(x, decay)

            def combine(c1, c2):
                a1, b1 = c1
                a2, b2 = c2
                return (a1 * a2, a2 * b1 + b2)
            _, y = jax.lax.associative_scan(combine, (a, x), axis=1)
            return y
        scale = jnp.float32(np.sqrt(1.0 - DECAY))
        gate = jax.nn.sigmoid(jnp.einsum('bse,em->bsm', x, Wg) + bg)
        store = jnp.einsum('bse,em->bsm', x, Wv) * gate * scale
        mem = smear(store, DECAY)
        que = jax.nn.sigmoid(jnp.einsum('bse,em->bsm', x, Wq) + bq)
        load = mem * que * scale
        return jnp.einsum('bsm,me->bse', load, Wo)

    def _L0_ffn_ref(x, weight, scale, expert_masks, router_w):
        import jax, jax.numpy as jnp
        import numpy as np
        B, S, D_IN, D_OUT, E = (4, 128, 256, 256, 32)
        MASK_DENSITY = 0.3
        THRESH = 0.5
        logits = jnp.einsum('bsd,ed->bse', x, router_w)
        probs = jax.nn.softmax(logits, axis=-1)
        top1_w = jnp.max(probs, axis=-1)
        top1_idx = jnp.argmax(probs, axis=-1)
        w_q = jnp.clip(jnp.round(weight / THRESH), -1.0, 1.0)
        w_scaled = w_q * scale[:, None]
        out0 = jnp.zeros((x.shape[0], x.shape[1], weight.shape[0]), dtype=x.dtype)

        def body(out, inputs):
            e_idx, mask_e = inputs
            y = jnp.einsum('bsi,oi->bso', x, w_scaled * mask_e)
            sel = (top1_idx == e_idx)[..., None]
            out = jnp.where(sel, y * top1_w[..., None], out)
            return (out, None)
        out, _ = jax.lax.scan(body, out0, (jnp.arange(E), expert_masks))
        return out
    x = L0_attn_x
    x = x + 0.5 * _L0_ffn_ref(_layernorm(x, axis=-1), L0_ffn_weight, L0_ffn_scale, L0_ffn_expert_masks, L0_ffn_router_w)
    x = x + _L0_attn_ref(_layernorm(x, axis=-1), L0_attn_Wv, L0_attn_Wg, L0_attn_bg, L0_attn_Wq, L0_attn_bq, L0_attn_Wo)
    x = x + 0.5 * _L0_ffn_ref(_layernorm(x, axis=-1), L0_ffn_weight, L0_ffn_scale, L0_ffn_expert_masks, L0_ffn_router_w)
    return x

_drawn_inputs = setup_inputs


def setup_inputs(seed=0):
    import zlib

    import numpy as np

    out = dict(_drawn_inputs(seed))
    spreads = {'L0_attn_bg': (0.0, 0.8), 'L0_attn_bq': (0.0, 0.8), 'L0_ffn_scale': (1.0, 0.2)}
    factors = {'L0_attn_Wv': 8.0, 'L0_attn_Wg': 8.0, 'L0_attn_Wq': 8.0, 'L0_attn_Wo': 8.0}
    for name, (base, spread) in spreads.items():
        noise = np.random.default_rng([zlib.crc32(name.encode()), seed]).standard_normal(out[name].shape)
        drawn = base * np.exp(spread * noise) if base else spread * noise
        out[name] = jnp.asarray(drawn.astype(out[name].dtype))
    for name, factor in factors.items():
        out[name] = (out[name] * factor).astype(out[name].dtype)
    return out
```

```python
from contextlib import ExitStack

import numpy as np
import concourse.bass as bass
from concourse import mybir

F32 = mybir.dt.float32
BF16 = mybir.dt.bfloat16
I32 = mybir.dt.int32
U32 = mybir.dt.uint32
ALU = mybir.AluOpType
ACT = mybir.ActivationFunctionType
AX = mybir.AxisListType

P = 128
EPS = 1e-5
DECAY = 0.95
THRESH = 0.5
TILES_PER_GROUP = 4
CHUNK = 4
BODY = 2 * CHUNK


def macaron_block(nc, x, wv, wg, bg, wq, bq, wo, weight, scale, masks, router, out):
    B, S, D = x.shape
    E = masks.shape[0]
    TOKENS = B * S
    TILES = TOKENS // P
    J = TILES_PER_GROUP
    GROUPS = TILES // J
    GT = J * P
    SEQS = GT // S
    KC = D // P
    ROUNDS = TOKENS // P
    SKIP = 1 << 16
    CHUNKS = E // CHUNK
    GATE = float(np.float32(np.sqrt(1.0 - DECAY))) ** 2 / 4
    assert D == KC * P and TILES == GROUPS * J and GT == SEQS * S and GT <= 512 and KC == 2
    assert E % BODY == 0 and J * E <= 128 and GROUPS == 4

    x_rows = x.rearrange("b s d -> (b s) d").rearrange("(t p) d -> p t d", p=P)
    out_rows = out.rearrange("b s d -> (b s) d").rearrange("(t p) d -> p t d", p=P)
    mask_rows = masks.rearrange("e o i -> (e o) i").rearrange("(n p) i -> p n i", p=P)

    xs_dram = nc.dram_tensor("rows_by_expert", (E * P, D), F32, kind="Internal").ap()
    ys_dram = nc.dram_tensor("results_by_expert", (E * P, D), F32, kind="Internal").ap()
    xs_tiles = xs_dram.rearrange("(e p) d -> p e d", p=P)
    ys_tiles = ys_dram.rearrange("(e p) d -> p e d", p=P)
    LAST_ROW = E * P - 1

    with ExitStack() as ctx:
        def sb(name, shape, dt=F32):
            return ctx.enter_context(nc.sbuf_tensor(name, shape, dt))

        def psum(name):
            return ctx.enter_context(nc.psum_tensor(name, [P, 512], F32))

        def sem(name):
            return ctx.enter_context(nc.semaphore(name))

        w_exp = sb("w_exp", [P, E, KC, D])
        xs = sb("xs", [P, BODY, D])
        ys = sb("ys", [P, BODY, D])
        zeros = sb("zeros", [P, BODY, D])
        xt = sb("xt", [P, TILES, D])
        xf = sb("xf", [P, TILES, D])
        xa = sb("xa", [P, J, D])
        xfT = sb("xfT", [P, KC, GT])
        xaT = sb("xaT", [P, GROUPS, KC, GT])
        mask_raw = xaT[:, :, :, :].rearrange("p a b c -> p (a b c)").rearrange(
            "p (s n i) -> p s n i", s=2, i=D)
        xsT = sb("xsT", [P, 2, KC, P])
        w_att = sb("w_att", [P, 3, KC, D])
        w_out = sb("w_out", [P, KC, D])
        tanh_g = sb("tanh_g", [P, KC, GT])
        tanh_q = sb("tanh_q", [P, KC, GT])
        store = sb("store", [P, KC, GT])
        mem = sb("mem", [P, KC, GT])
        load = sb("load", [P, KC, GT])
        w_nat = sb("w_nat", [P, KC, D])
        w_low = sb("w_low", [P, KC, D])
        w_qs = sb("w_qs", [P, KC, D])
        w_qsT = sb("w_qsT", [P, KC, D])
        r_nat = sb("r_nat", [E, D])
        rT = sb("rT", [P, KC, E])
        vec_rows = sb("vec_rows", [6, P])
        vecs = sb("vecs", [P, 6])
        half_b = sb("half_b", [P, 4])
        ident = sb("ident", [P, P])
        ones_f = sb("ones_f", [P, P])
        below = sb("below", [P, P], BF16)
        ones = sb("ones", [P, P], BF16)
        iota_e = sb("iota_e", [P, E], I32)
        expert = sb("expert", [P, E], BF16)
        prefer = sb("prefer", [P, J, E])
        decay = sb("decay", [P, S])
        neg_half = sb("neg_half", [P, J])
        NI = 3 * GROUPS
        stats = sb("stats", [P, NI, J, 6])
        mv = sb("mv", [P, NI, J, 2])
        var_eps = sb("var_eps", [P, NI, J])
        rstd = sb("rstd", [P, NI, J])
        nmr = sb("nmr", [P, NI, J])
        top = sb("top", [P, TILES])
        lm = sb("lm", [P, TILES, E])
        is_top = sb("is_top", [P, J, E])
        cand = sb("cand", [P, J, E])
        best = sb("best", [P, J])
        hot = sb("hot", [P, TILES, E], BF16)
        gsum = sb("gsum", [P, E])
        cum = sb("cum", [P, GROUPS + 1, E], BF16)
        pos = sb("pos", [P, J, E])
        slot = sb("slot", [P, TILES])
        limit = sb("limit", [P, TILES])
        late = sb("late", [P, TILES])
        early = sb("early", [P, TILES])
        row = sb("row", [P, TILES], U32)
        esum = sb("esum", [P, TILES])
        prob = sb("prob", [P, TILES])
        half_w = sb("half_w", [P, TILES])
        most = sb("most", [P, 2])
        flag = sb("flag", [P, 2], I32)

        XT = [psum("XT0"), psum("XT1")]
        PJ = [psum("PG"), psum("PV"), psum("PQ")]
        O = [psum("O0"), psum("O1")]
        RT = psum("RT")
        LG = RT[:, 0:J * E]
        RK = RT[:, J * E:2 * J * E]
        CN = RT[:, 2 * J * E:2 * J * E + E]

        x_first, x_rest = sem("x_first"), sem("x_rest")
        w_in, small_in, att_in = sem("w_in"), sem("small_in"), sem("att_in")
        mask_in = [sem("mask_in0"), sem("mask_in1")]
        zero_src, zeroed = sem("zero_src"), sem("zeroed")
        iota_done, ident_done, ones_f_done, below_done = (sem("iota_done"), sem("ident_done"),
                                                          sem("ones_f_done"), sem("below_done"))
        ones_done, consts_done, neg_half_done = sem("ones_done"), sem("consts_done"), sem("neg_half_done")
        small_T, small_ready, low_done, quant_done = (sem("small_T"), sem("small_ready"),
                                                      sem("low_done"), sem("quant_done"))
        qs_done, qsT_full, qsT_ready, att_ready = (sem("qs_done"), sem("qsT_full"),
                                                   sem("qsT_ready"), sem("att_ready"))
        mask_T, w_ready = sem("mask_T"), sem("w_ready")
        ln = {k: {s: sem(f"ln{k}_{s}") for s in ("stats", "mv", "var", "rstd", "nmr", "xn")} for k in "FA"}
        xt_full, xt_out = sem("xt_full"), sem("xt_out")
        lg_ready, top_done, lg_read, cand_done = (sem("lg_ready"), sem("top_done"),
                                                  sem("lg_read"), sem("cand_done"))
        best_done, hot_done, gsum_done, cum_done = (sem("best_done"), sem("hot_done"),
                                                    sem("gsum_done"), sem("cum_done"))
        slot_done, late_done = sem("slot_done"), sem("late_done")
        rk_ready, pos_done, row_done, scattered = (sem("rk_ready"), sem("pos_done"),
                                                   sem("row_done"), sem("scattered"))
        cn_ready, most_done, flag_done = sem("cn_ready"), sem("most_done"), sem("flag_done")
        exp_done, esum_done, prob_done, half_done = (sem("exp_done"), sem("esum_done"),
                                                     sem("prob_done"), sem("half_done"))
        xs_in = [sem("xs_in0"), sem("xs_in1")]
        y_full, y_out, ys_written = sem("y_full"), sem("y_out"), [sem("ys_written0"), sem("ys_written1")]
        gathered = [sem(f"gathered{g}") for g in range(GROUPS)]
        x1_done, x2_done, x3_done, out_written = (sem("x1_done"), sem("x2_done"),
                                                  sem("x3_done"), sem("out_written"))
        pg_ready, pv_ready, pq_ready = sem("pg_ready"), sem("pv_ready"), sem("pq_ready")
        tg_done, tq_done, st_done, mem_done, ld_done = (sem("tg_done"), sem("tq_done"), sem("st_done"),
                                                        sem("mem_done"), sem("ld_done"))
        o_ready = sem("o_ready")
        ov = [{s: sem(f"over{L}_{s}") for s in ("free", "step", "cur", "edge", "row", "scat", "gath", "in", "T", "xsT", "y", "yout", "st")}
              for L in range(2)]

        XT_EXP = [2 * GROUPS, 2 * GROUPS + E + 4 * GROUPS]
        XT_MEM = 2 * GROUPS + E

        def xt_attn(g):
            return XT_MEM + (2 * g if g < 2 else 4 * g - 2)

        def xt_ffn(L, g):
            if L == 0:
                return 2 * g
            if g == GROUPS - 1:
                return XT_MEM + 4 * GROUPS - 2
            return XT_MEM + 4 + 4 * g

        def tiles(g):
            return slice(g * J, (g + 1) * J)

        block = ctx.enter_context(nc.Block())

        @block.sync
        def _(sp):
            sp.dma_start(xt[:, 0:J, :], x_rows[:, 0:J, :]).then_inc(x_first, 16)
            sp.dma_start(r_nat[:, :], router).then_inc(small_in, 16)
            for k, v in enumerate((bg, bq, scale)):
                sp.dma_start(vec_rows[2 * k:2 * k + 2, :], v.rearrange("(c p) -> c p", p=P)).then_inc(small_in, 16)
            for g in range(1, GROUPS):
                sp.dma_start(xt[:, g * J:(g + 1) * J, :], x_rows[:, g * J:(g + 1) * J, :]).then_inc(x_rest, 16)
            sp.dma_start(w_nat[:, :, :], weight.rearrange("(c p) i -> p c i", p=P)).then_inc(w_in, 16)
            sp.wait_ge(zero_src, 1)
            for c in range(E // BODY):
                sp.dma_start(xs_tiles[:, c * BODY:(c + 1) * BODY, :], zeros[:, :, :]).then_inc(zeroed, 16)
            for c in range(2):
                sp.dma_start(mask_raw[:, c], mask_rows[:, c * KC * CHUNK:(c + 1) * KC * CHUNK, :]).then_inc(mask_in[c], 16)
            for k, w in enumerate((wg, wv, wq)):
                sp.dma_start(w_att[:, k], w.rearrange("(c p) m -> p c m", p=P)).then_inc(att_in, 16)
            sp.dma_start(w_out[:, :, :], wo.rearrange("(c p) m -> p c m", p=P)).then_inc(att_in, 16)

            def load_rows(c, b):
                sp.dma_start(xs[:, b * CHUNK:(b + 1) * CHUNK, :],
                             xs_tiles[:, bass.ds(c * CHUNK, CHUNK), :]).then_inc(xs_in[b], 16)

            def load_masks(c, b):
                sp.dma_start(mask_raw[:, b],
                             mask_rows[:, bass.ds(c * KC * CHUNK, KC * CHUNK), :]).then_inc(mask_in[b], 16)

            def store_results(L, c, b):
                sp.wait_ge(y_out, E * L + CHUNK * (c + 1))
                sp.dma_start(ys_tiles[:, bass.ds(c * CHUNK, CHUNK), :],
                             ys[:, b * CHUNK:(b + 1) * CHUNK, :]).then_inc(ys_written[b], 16)

            for L in range(2):
                sp.wait_ge(scattered, 16 * TILES * (L + 1))
                if L == 0:
                    sp.wait_ge(zeroed, 16 * (E // BODY))
                load_rows(0, 0)
                load_rows(1, 1)
                with sp.Fori(0, CHUNKS // 2 - 1) as i:
                    for b in range(2):
                        c = 2 * i + b
                        sp.wait_ge(xt_full, XT_EXP[L] + CHUNK * (c + 1))
                        load_rows(c + 2, b)
                        if L == 0:
                            load_masks(c + 2, b)
                        store_results(L, c, b)
                for c in range(CHUNKS - 2, CHUNKS):
                    store_results(L, c, c % 2)

                sp.wait_ge(flag_done, L + 1)
                over = sp.value_load(flag[0:1, L:L + 1], min_val=0, max_val=1)
                with sp.If(over > 0):
                    v = ov[L]
                    for g in range(GROUPS):
                        sp.wait_ge(gathered[g], 16 * J * (L + 1))
                    with sp.Fori(0, ROUNDS - 1) as r:
                        with sp.Fori(0, E) as e:
                            sp.wait_ge(v["scat"], 16 * TILES * (r + 1))
                            sp.dma_start(xs[:, 0:1, :], xs_tiles[:, bass.ds(e, 1), :]).then_inc(v["in"], 16)
                            sp.wait_ge(v["yout"], r * E + e + 1)
                            sp.dma_start(ys_tiles[:, bass.ds(e, 1), :], ys[:, 0:1, :]).then_inc(v["st"], 16)

            for g in range(GROUPS):
                sp.wait_ge(x3_done, J * (g + 1))
                sp.dma_start(out_rows[:, g * J:(g + 1) * J, :], xt[:, g * J:(g + 1) * J, :]).then_inc(out_written, 16)
            sp.wait_ge(out_written, 16 * GROUPS)

        @block.gpsimd
        def _(pool):
            pool.memset(ones_f[:, :], 1.0).then_inc(ones_f_done, 1)
            pool.memset(neg_half[:, :], -0.5).then_inc(neg_half_done, 1)
            pool.wait_ge(ones_f_done, 1)
            pool.affine_select(out=ident[:, :], in_=ones_f[:, :], pattern=[[1, P]], compare_op=ALU.is_equal,
                               fill=0.0, base=0, channel_multiplier=-1).then_inc(ident_done, 1)
            pool.iota(iota_e[:, :], pattern=[[1, E]], base=0, channel_multiplier=0).then_inc(iota_done, 1)
            pool.memset(zeros[:, :, :], 0.0).then_inc(zero_src, 1)
            pool.wait_ge(ones_done, 1)
            pool.affine_select(out=below[:, :], in_=ones[:, :], pattern=[[1, P]], compare_op=ALU.is_gt,
                               fill=0.0, base=0, channel_multiplier=-1).then_inc(below_done, 1)

            def inv_std(kind, n, q):
                pool.wait_ge(ln[kind]["var"], n + 1)
                pool.tensor_tensor(rstd[:, q, :], var_eps[:, q, :],
                                   neg_half[:, :], ALU.pow).then_inc(ln[kind]["rstd"], 1)

            def scatter(L, g):
                n = L * GROUPS + g
                pool.wait_ge(row_done, n + 1)
                pool.wait_ge(ln["F"]["xn"], J * (n + 1))
                for t in range(g * J, (g + 1) * J):
                    pool.indirect_dma_start(xs_dram, bass.IndirectOffsetOnAxis(ap=row[:, t:t + 1], axis=0),
                                            xf[:, t, :], None, bounds_check=LAST_ROW, oob_is_err=False
                                            ).then_inc(scattered, 16)

            def gather(L):
                for b in range(2):
                    pool.wait_ge(ys_written[b], 16 * CHUNKS // 2 * (L + 1))
                for t in range(TILES):
                    pool.indirect_dma_start(xf[:, t, :], None, ys_dram,
                                            bass.IndirectOffsetOnAxis(ap=row[:, t:t + 1], axis=0),
                                            bounds_check=LAST_ROW, oob_is_err=False).then_inc(gathered[t // J], 16)
                pool.wait_ge(flag_done, L + 1)
                over = pool.value_load(flag[0:1, L:L + 1], min_val=0, max_val=1)
                with pool.If(over > 0):
                    v = ov[L]
                    for g in range(GROUPS):
                        pool.wait_ge(gathered[g], 16 * J * (L + 1))
                    pool.sem_inc(v["free"], 1)
                    with pool.Fori(0, ROUNDS - 1) as r:
                        pool.wait_ge(v["row"], r + 1)
                        pool.sem_inc(v["step"], 1)
                        for t in range(TILES):
                            pool.indirect_dma_start(xs_dram, bass.IndirectOffsetOnAxis(ap=row[:, t:t + 1], axis=0),
                                                    xf[:, t, :], None, bounds_check=LAST_ROW, oob_is_err=False
                                                    ).then_inc(v["scat"], 16)
                        pool.wait_ge(v["st"], 16 * E * (r + 1))
                        pool.sem_inc(v["step"], 1)
                        for t in range(TILES):
                            pool.indirect_dma_start(xf[:, t, :], None, ys_dram,
                                                    bass.IndirectOffsetOnAxis(ap=row[:, t:t + 1], axis=0),
                                                    bounds_check=LAST_ROW, oob_is_err=False).then_inc(v["gath"], 16)

            inv_std("F", 0, 0)
            pool.wait_ge(zeroed, 16 * (E // BODY))
            for g in range(GROUPS - 1):
                inv_std("F", g + 1, g + 1)
                scatter(0, g)
            scatter(0, GROUPS - 1)
            gather(0)
            QA = 2 * GROUPS
            inv_std("A", 0, QA)
            inv_std("A", 1, QA + 1)
            for i in range(1, GROUPS - 1):
                inv_std("A", i + 1, QA + 1 + i)
                inv_std("F", GROUPS + i - 1, GROUPS + i - 1)
                scatter(1, i - 1)
            for g in (GROUPS - 2, GROUPS - 1):
                inv_std("F", GROUPS + g, GROUPS + g)
                scatter(1, g)
            gather(1)

        @block.scalar
        def _(act):
            def normalise(kind, n, q, t0, dst):
                act.wait_ge(ln[kind]["nmr"], n + 1)
                for j in range(J):
                    act.activation(dst(j), xt[:, t0 + j, :], ACT.Identity,
                                   bias=nmr[:, q, j:j + 1],
                                   scale=rstd[:, q, j:j + 1]
                                   ).then_inc(ln[kind]["xn"], 1)

            def normalise_ffn(L, g):
                n = L * GROUPS + g
                if L == 1:
                    act.wait_ge(x1_done, J * (g + 1))
                normalise("F", n, n, g * J, lambda j: xf[:, g * J + j, :])

            def normalise_mem(g):
                if g > 0:
                    act.wait_ge(xt_full, xt_attn(g - 1) + 2)
                normalise("A", g, 2 * GROUPS + g, g * J, lambda j: xa[:, j, :])

            def copy_T(u, dst):
                for h in range(2):
                    act.wait_ge(xt_full, u + h + 1)
                    act.copy(dst[:, :, h * 2 * P:(h + 1) * 2 * P].rearrange("p k (j c) -> p k j c", j=2),
                             XT[h][:, :].rearrange("p (j k c) -> p k j c", j=2, k=KC)).then_inc(xt_out, 1)

            def copy_T_ffn(L, g):
                n = L * GROUPS + g
                if n > 0:
                    act.wait_ge(lg_ready, n)
                copy_T(xt_ffn(L, g), xfT)

            def copy_T_mem(g):
                copy_T(xt_attn(g), xaT[:, g])

            def exponentials(L):
                act.wait_ge(lg_read, 2 * GROUPS * (L + 1))
                act.activation(lm[:, :, :], lm[:, :, :], ACT.Exp).then_inc(exp_done, 1)

            def experts(L):
                with act.Fori(0, CHUNKS // 2) as i:
                    for s in range(2):
                        if L == 0:
                            act.wait_ge(ys_written[s], 16 * i)
                        for m in range(CHUNK):
                            e, b = BODY * i + CHUNK * s + m, m % 2
                            act.wait_ge(xt_full, XT_EXP[L] + e + 1)
                            if L == 1 or s + m > 0:
                                act.wait_ge(y_full, E * L + e - 1)
                            else:
                                act.wait_ge(y_full, BODY * i)
                            act.copy(xsT[:, b], XT[b][:, 0:KC * P].rearrange("p (k c) -> p k c", k=KC)
                                     ).then_inc(xt_out, 1)
                            if L == 0:
                                act.wait_ge(y_full, e + 1)
                                act.copy(ys[:, CHUNK * s + m, :], O[b][:, 0:D]).then_inc(y_out, 1)

            def overflow(L):
                act.wait_ge(flag_done, L + 1)
                over = act.value_load(flag[0:1, L:L + 1], min_val=0, max_val=1)
                with act.If(over > 0):
                    v = ov[L]
                    for b in range(2):
                        act.wait_ge(ys_written[b], 16 * CHUNKS // 2 * (L + 1))
                    with act.Fori(0, (ROUNDS - 1) * E) as n:
                        act.wait_ge(v["T"], n + 1)
                        act.copy(xsT[:, 0], XT[0][:, 0:KC * P].rearrange("p (k c) -> p k c", k=KC)).then_inc(v["xsT"], 1)
                        act.wait_ge(v["y"], n + 1)
                        act.wait_ge(v["st"], 16 * n)
                        act.copy(ys[:, 0, :], O[0][:, 0:D]).then_inc(v["yout"], 1)

            def tanhs(g):
                for c in range(KC):
                    n = KC * g + c
                    act.wait_ge(pg_ready, n + 1)
                    act.wait_ge(st_done, KC * g)
                    act.activation(tanh_g[:, c, :], PJ[0][:, 0:GT], ACT.Tanh, bias=half_b[:, c:c + 1],
                                   scale=0.5).then_inc(tg_done, 1)
                    act.wait_ge(pq_ready, n + 1)
                    act.wait_ge(ld_done, KC * g)
                    act.activation(tanh_q[:, c, :], PJ[2][:, 0:GT], ACT.Tanh, bias=half_b[:, 2 + c:3 + c],
                                   scale=0.5).then_inc(tq_done, 1)

            normalise_ffn(0, 0)
            for g in range(GROUPS - 1):
                normalise_ffn(0, g + 1)
                copy_T_ffn(0, g)
            copy_T_ffn(0, GROUPS - 1)
            exponentials(0)
            experts(0)
            overflow(0)

            normalise_mem(0)
            copy_T_mem(0)
            normalise_mem(1)
            tanhs(0)
            copy_T_mem(1)
            for i in range(1, GROUPS - 1):
                normalise_mem(i + 1)
                normalise_ffn(1, i - 1)
                tanhs(i)
                copy_T_ffn(1, i - 1)
                copy_T_mem(i + 1)
            normalise_ffn(1, GROUPS - 2)
            tanhs(GROUPS - 1)
            copy_T_ffn(1, GROUPS - 2)
            normalise_ffn(1, GROUPS - 1)
            copy_T_ffn(1, GROUPS - 1)
            exponentials(1)
            experts(1)
            overflow(1)

        @block.vector
        def _(dve):
            def norm_stats(kind, n, q, t0):
                s = ln[kind]
                for j in range(J):
                    dve.bn_stats(stats[:, q, j, :], xt[:, t0 + j, :]).then_inc(s["stats"], 1)
                for j in range(J):
                    dve.wait_ge(s["stats"], J * n + j + 1)
                    dve.bn_aggr(mv[:, q, j, :], stats[:, q, j, :]).then_inc(s["mv"], 1)
                dve.wait_ge(s["mv"], J * (n + 1))
                dve.tensor_scalar(var_eps[:, q, :], mv[:, q, :, 1], EPS, None,
                                  ALU.add).then_inc(s["var"], 1)

            def norm_bias(kind, n, q):
                dve.wait_ge(ln[kind]["rstd"], n + 1)
                dve.scalar_tensor_tensor(out=nmr[:, q, :], in0=mv[:, q, :, 0], scalar=-1.0,
                                         in1=rstd[:, q, :], op0=ALU.mult,
                                         op1=ALU.mult).then_inc(ln[kind]["nmr"], 1)

            def choose(L, g):
                n = L * GROUPS + g
                lg = LG.rearrange("p (j e) -> p j e", j=J)
                top_b = top[:, tiles(g)].unsqueeze(2).to_broadcast([P, J, E])
                dve.wait_ge(lg_ready, n + 1)
                dve.tensor_reduce(top[:, tiles(g)], lg, AX.X, ALU.max).then_inc(top_done, 1)
                dve.wait_ge(top_done, n + 1)
                dve.tensor_tensor(is_top[:, :, :], lg, top_b, ALU.is_equal).then_inc(lg_read, 1)
                dve.tensor_tensor(lm[:, tiles(g), :], lg, top_b, ALU.subtract).then_inc(lg_read, 1)
                dve.wait_ge(lg_read, 2 * n + 1)
                dve.tensor_tensor(cand[:, :, :], is_top[:, :, :], prefer[:, :, :], ALU.mult).then_inc(cand_done, 1)
                dve.wait_ge(cand_done, n + 1)
                dve.tensor_reduce(best[:, :], cand[:, :, :], AX.X, ALU.max).then_inc(best_done, 1)
                dve.wait_ge(best_done, n + 1)
                dve.tensor_tensor(hot[:, tiles(g), :], cand[:, :, :],
                                  best[:, :].unsqueeze(2).to_broadcast([P, J, E]), ALU.is_equal).then_inc(hot_done, 1)
                dve.wait_ge(hot_done, n + 1)
                dve.tensor_reduce(gsum[:, :], hot[:, tiles(g), :].rearrange("p j e -> p e j"), AX.X,
                                  ALU.add).then_inc(gsum_done, 1)
                dve.wait_ge(gsum_done, n + 1)
                if n > 0:
                    dve.wait_ge(cum_done, n)
                dve.tensor_tensor(cum[:, g + 1, :],
                                  cum[:, g, :], gsum[:, :],
                                  ALU.add).then_inc(cum_done, 1)

            def number(L, g):
                n = L * GROUPS + g
                dve.wait_ge(rk_ready, n + 1)
                dve.tensor_tensor(pos[:, :, :], hot[:, tiles(g), :], RK.rearrange("p (j e) -> p j e", j=J),
                                  ALU.mult).then_inc(pos_done, 1)
                dve.wait_ge(pos_done, n + 1)
                dve.tensor_reduce(slot[:, tiles(g)], pos[:, :, :], AX.X, ALU.add).then_inc(slot_done, 1)
                dve.tensor_scalar(limit[:, tiles(g)], best[:, :], -float(P), float((E + 1) * P), ALU.mult,
                                  ALU.add).then_inc(slot_done, 1)
                dve.wait_ge(slot_done, 2 * (n + 1))
                dve.tensor_tensor(late[:, tiles(g)], slot[:, tiles(g)], limit[:, tiles(g)],
                                  ALU.is_ge).then_inc(late_done, 1)
                dve.wait_ge(late_done, n + 1)
                dve.scalar_tensor_tensor(out=row[:, tiles(g)], in0=late[:, tiles(g)], scalar=float(SKIP),
                                         in1=slot[:, tiles(g)], op0=ALU.mult, op1=ALU.add).then_inc(row_done, 1)

            def overflow_flag(L):
                dve.wait_ge(cn_ready, L + 1)
                dve.tensor_reduce(most[:, L:L + 1], CN, AX.X, ALU.max).then_inc(most_done, 1)
                dve.wait_ge(most_done, L + 1)
                dve.tensor_scalar(flag[:, L:L + 1], most[:, L:L + 1], float(P), None,
                                  ALU.is_gt).then_inc(flag_done, 1)

            def overflow(L):
                over = dve.value_load(flag[0:1, L:L + 1], min_val=0, max_val=1)
                with dve.If(over > 0):
                    v = ov[L]
                    dve.wait_ge(v["free"], 1)
                    with dve.Fori(0, ROUNDS - 1) as r:
                        dve.wait_ge(v["row"], r)
                        dve.tensor_scalar(slot[:, :], slot[:, :], -float(P), None, ALU.add).then_inc(v["cur"], 1)
                        dve.wait_ge(v["cur"], r + 1)
                        dve.tensor_tensor(late[:, :], slot[:, :], limit[:, :], ALU.is_ge).then_inc(v["edge"], 1)
                        dve.scalar_tensor_tensor(out=early[:, :], in0=slot[:, :], scalar=float(P), in1=limit[:, :],
                                                 op0=ALU.add, op1=ALU.is_lt).then_inc(v["edge"], 1)
                        dve.wait_ge(v["edge"], 3 * r + 2)
                        dve.tensor_tensor(late[:, :], late[:, :], early[:, :], ALU.add).then_inc(v["edge"], 1)
                        dve.wait_ge(v["edge"], 3 * r + 3)
                        dve.wait_ge(v["gath"], 16 * TILES * r)
                        dve.scalar_tensor_tensor(out=row[:, :], in0=late[:, :], scalar=float(SKIP), in1=slot[:, :],
                                                 op0=ALU.mult, op1=ALU.add).then_inc(v["row"], 1)
                    dve.wait_ge(v["gath"], 16 * TILES * (ROUNDS - 1))

            def top_weights(L):
                dve.wait_ge(exp_done, L + 1)
                dve.tensor_reduce(esum[:, :], lm[:, :, :], AX.X, ALU.add).then_inc(esum_done, 1)
                dve.wait_ge(esum_done, L + 1)
                dve.reciprocal(prob[:, :], esum[:, :]).then_inc(prob_done, 1)
                dve.wait_ge(prob_done, L + 1)
                dve.tensor_scalar(half_w[:, :], prob[:, :], 0.5, None, ALU.mult).then_inc(half_done, 1)

            def add_ffn(L, g, done):
                s = gathered[g]
                dve.wait_ge(s, 16 * J * (L + 1))
                dve.wait_ge(half_done, L + 1)
                for j in range(J):
                    t = g * J + j
                    dve.scalar_tensor_tensor(out=xt[:, t, :], in0=xf[:, t, :], scalar=half_w[:, t:t + 1], in1=xt[:, t, :],
                                             op0=ALU.mult, op1=ALU.add).then_inc(done, 1)

            def add_and_norm_mem(g):
                add_ffn(0, g, x1_done)
                dve.wait_ge(x1_done, J * (g + 1))
                norm_stats("A", g, 2 * GROUPS + g, g * J)
                norm_bias("A", g, 2 * GROUPS + g)

            def memory(g):
                for c in range(KC):
                    n = KC * g + c
                    dve.wait_ge(tg_done, n + 1)
                    dve.wait_ge(pv_ready, n + 1)
                    dve.scalar_tensor_tensor(out=store[:, c, :], in0=tanh_g[:, c, :], scalar=1.0,
                                             in1=PJ[1][:, 0:GT], op0=ALU.add, op1=ALU.mult).then_inc(st_done, 1)
                    dve.wait_ge(st_done, n + 1)
                    for h in range(SEQS):
                        s = slice(h * S, (h + 1) * S)
                        dve.tensor_tensor_scan(mem[:, c, s], decay[:, :], store[:, c, s], 0.0, ALU.mult,
                                               ALU.add).then_inc(mem_done, 1)
                    dve.wait_ge(tq_done, n + 1)
                    dve.wait_ge(mem_done, SEQS * (n + 1))
                    dve.wait_ge(o_ready, J * g)
                    dve.scalar_tensor_tensor(out=load[:, c, :], in0=tanh_q[:, c, :], scalar=1.0, in1=mem[:, c, :],
                                             op0=ALU.add, op1=ALU.mult).then_inc(ld_done, 1)

            def add_mem_and_norm(g):
                for j in range(J):
                    t = g * J + j
                    dve.wait_ge(o_ready, J * g + j + 1)
                    dve.tensor_tensor(xt[:, t, :], xt[:, t, :], O[j % 2][:, 0:D],
                                      ALU.add).then_inc(x2_done, 1)
                dve.wait_ge(x2_done, J * (g + 1))
                norm_stats("F", GROUPS + g, GROUPS + g, g * J)
                norm_bias("F", GROUPS + g, GROUPS + g)

            dve.memset(ones[:, :], 1.0).then_inc(ones_done, 1)
            dve.memset(decay[:, :], DECAY).then_inc(consts_done, 1)
            dve.memset(cum[:, 0, :], 0.0).then_inc(consts_done, 1)
            dve.wait_ge(iota_done, 1)
            dve.tensor_copy(expert[:, :], iota_e[:, :]).then_inc(consts_done, 1)
            dve.tensor_scalar(prefer[:, :, :], iota_e[:, :].unsqueeze(1).to_broadcast([P, J, E]), -1.0, float(E),
                              ALU.mult, ALU.add).then_inc(consts_done, 1)

            dve.wait_ge(x_first, 16)
            norm_stats("F", 0, 0, 0)
            dve.wait_ge(small_T, 1)
            dve.tensor_copy(rT[:, :, :], PJ[0][:, 0:KC * E].rearrange("p (k e) -> p k e", k=KC)).then_inc(small_ready, 1)
            dve.tensor_copy(vecs[:, :], PJ[0][:, KC * E:KC * E + 6]).then_inc(small_ready, 1)
            norm_bias("F", 0, 0)
            dve.wait_ge(w_in, 16)
            dve.tensor_scalar(w_low[:, :, :], w_nat[:, :, :], -THRESH / 2, None, ALU.is_lt).then_inc(low_done, 1)
            dve.wait_ge(low_done, 1)
            dve.scalar_tensor_tensor(out=w_qs[:, :, :], in0=w_nat[:, :, :], scalar=THRESH / 2, in1=w_low[:, :, :],
                                     op0=ALU.is_gt, op1=ALU.subtract).then_inc(quant_done, 1)
            dve.wait_ge(quant_done, 1)
            dve.wait_ge(small_ready, 2)
            for c in range(KC):
                dve.tensor_scalar(w_low[:, c, :], w_qs[:, c, :], vecs[:, 4 + c:5 + c], None,
                                  ALU.mult).then_inc(qs_done, 1)

            dve.wait_ge(consts_done, 4)
            dve.wait_ge(x_rest, 16 * (GROUPS - 1))
            for g in range(GROUPS - 1):
                norm_stats("F", g + 1, g + 1, (g + 1) * J)
                norm_bias("F", g + 1, g + 1)
                choose(0, g)
                number(0, g)
            choose(0, GROUPS - 1)
            number(0, GROUPS - 1)
            overflow_flag(0)
            dve.wait_ge(qsT_full, 1)
            dve.tensor_copy(w_qsT[:, :, :], PJ[2][:, :].rearrange("p (k o) -> p k o", k=KC)).then_inc(qsT_ready, 1)
            dve.wait_ge(att_in, 64)
            dve.tensor_scalar(half_b[:, :], vecs[:, 0:4], 0.5, None, ALU.mult).then_inc(att_ready, 1)
            dve.tensor_scalar(w_out[:, :, :], w_out[:, :, :], GATE, None, ALU.mult).then_inc(att_ready, 1)
            dve.wait_ge(qsT_ready, 1)
            with dve.Fori(0, E // 2) as i:
                for b in range(2):
                    e = 2 * i + b
                    dve.wait_ge(mask_T, e + 1)
                    dve.tensor_tensor(w_exp[:, bass.ds(e, 1), :, :].rearrange("p a k o -> p (a k) o"),
                                      PJ[b][:, :].rearrange("p (k o) -> p k o", k=KC), w_qsT[:, :, :],
                                      ALU.mult).then_inc(w_ready, 1)
            top_weights(0)
            overflow(0)

            add_and_norm_mem(0)
            add_and_norm_mem(1)
            memory(0)
            for i in range(1, GROUPS - 1):
                add_and_norm_mem(i + 1)
                add_mem_and_norm(i - 1)
                memory(i)
                choose(1, i - 1)
                number(1, i - 1)
            add_mem_and_norm(GROUPS - 2)
            memory(GROUPS - 1)
            choose(1, GROUPS - 2)
            number(1, GROUPS - 2)
            add_mem_and_norm(GROUPS - 1)
            choose(1, GROUPS - 1)
            number(1, GROUPS - 1)
            overflow_flag(1)
            top_weights(1)
            with dve.Fori(0, CHUNKS // 2) as i:
                for s in range(2):
                    dve.wait_ge(ys_written[s], 16 * (CHUNKS // 2 + i))
                    for m in range(CHUNK):
                        dve.wait_ge(y_full, E + BODY * i + CHUNK * s + m + 1)
                        dve.tensor_copy(ys[:, CHUNK * s + m, :], O[m % 2][:, 0:D]).then_inc(y_out, 1)
            overflow(1)
            for g in range(GROUPS):
                add_ffn(1, g, x3_done)

        @block.tensor
        def _(pe):
            def transpose_group(kind, n, u, src):
                for h in range(2):
                    if u + h > 1:
                        pe.wait_ge(xt_out, u + h - 1)
                    for j in range(2):
                        pe.wait_ge(ln[kind]["xn"], J * n + 2 * h + j + 1)
                        for k in range(KC):
                            at = (j * KC + k) * P
                            ins = pe.transpose(XT[h][:, at:at + P], src(2 * h + j, k), ident[:, :])
                    ins.then_inc(xt_full, 1)

            def transpose_mem(g):
                transpose_group("A", g, xt_attn(g), lambda j, k: xa[:, j, k * P:(k + 1) * P])

            def transpose_ffn(L, g):
                transpose_group("F", L * GROUPS + g, xt_ffn(L, g),
                                lambda j, k: xf[:, g * J + j, k * P:(k + 1) * P])

            def logits(L, g):
                n = L * GROUPS + g
                u = xt_ffn(L, g)
                if n > 0:
                    pe.wait_ge(pos_done, n)
                if n == GROUPS:
                    pe.wait_ge(most_done, 1)
                for j in range(J):
                    pe.wait_ge(xt_out, u + j // 2 + 1)
                    for k in range(KC):
                        ins = pe.matmul(LG[:, j * E:(j + 1) * E], xfT[:, k, j * P:(j + 1) * P], rT[:, k, :],
                                        start=(k == 0), stop=(k == KC - 1))
                ins.then_inc(lg_ready, 1)

            def ranks(L, g):
                n = L * GROUPS + g
                pe.wait_ge(hot_done, n + 1)
                pe.wait_ge(lg_read, 2 * (n + 1))
                if n > 0:
                    pe.wait_ge(cum_done, n)
                rk = RK.rearrange("p (j e) -> p j e", j=J)
                pe.matmul(rk, below[:, :], hot[:, tiles(g), :], start=True, stop=False)
                for j in range(J - 1):
                    pe.matmul(rk[:, j + 1:J, :], ones[:, :],
                              hot[:, g * J + j:g * J + j + 1, :].to_broadcast([P, J - 1 - j, E]), start=False, stop=False)
                pe.matmul(rk, ones[:, :], cum[:, g:g + 1, :].to_broadcast([P, J, E]), start=False, stop=False)
                pe.matmul(rk, ones[:, :], expert[:, :].unsqueeze(1).to_broadcast([P, J, E]),
                          start=False, stop=True).then_inc(rk_ready, 1)

            def counts(L):
                pe.wait_ge(cum_done, GROUPS * (L + 1))
                pe.wait_ge(pos_done, GROUPS * (L + 1))
                pe.matmul(CN, ones[:, :], cum[:, GROUPS, :], start=True, stop=True).then_inc(cn_ready, 1)

            def expert_rows(L, e, slot, b):
                pe.wait_ge(xt_out, XT_EXP[L] + e - 1)
                for k in range(KC):
                    ins = pe.transpose(XT[b][:, k * P:(k + 1) * P], xs[:, slot, k * P:(k + 1) * P], ident[:, :])
                ins.then_inc(xt_full, 1)

            def expert_product(L, e, b):
                pe.wait_ge(xt_out, XT_EXP[L] + e + 1)
                if L == 0:
                    pe.wait_ge(w_ready, e + 1)
                for k in range(KC):
                    ins = pe.matmul(O[b][:, 0:D], xsT[:, b, k, :],
                                    w_exp[:, bass.ds(e, 1), k, :].rearrange("p a o -> p (a o)"),
                                    start=(k == 0), stop=(k == KC - 1))
                ins.then_inc(y_full, 1)

            def experts(L):
                with pe.Fori(0, CHUNKS // 2) as i:
                    for s in range(2):
                        c = 2 * i + s
                        if L == 0:
                            pe.wait_ge(mask_in[s], 16 * (i + 1))
                        pe.wait_ge(xs_in[s], 16 * (CHUNKS // 2 * L + i + 1))
                        for m in range(CHUNK):
                            e, b = c * CHUNK + m, m % 2
                            if L == 0:
                                if s == 0 and m < 2:
                                    pe.wait_ge(w_ready, CHUNK * 2 * i)
                                else:
                                    pe.wait_ge(w_ready, e - 1)
                                for cc in range(KC):
                                    for k in range(KC):
                                        at = k * D + cc * P
                                        ins = pe.transpose(PJ[b][:, at:at + P],
                                                           mask_raw[:, s, KC * m + cc, k * P:(k + 1) * P], ident[:, :])
                                ins.then_inc(mask_T, 1)
                            expert_rows(L, e, CHUNK * s + m, b)
                            if s == 0 and m == 0:
                                pe.wait_ge(y_out, E * L + CHUNK * 2 * i)
                            elif s == 0 and m == 1:
                                pe.wait_ge(y_out, E * L + CHUNK * 2 * i)
                            else:
                                pe.wait_ge(y_out, E * L + e - 1)
                            expert_product(L, e, b)

            def overflow(L):
                pe.wait_ge(flag_done, L + 1)
                over = pe.value_load(flag[0:1, L:L + 1], min_val=0, max_val=1)
                with pe.If(over > 0):
                    v = ov[L]
                    pe.wait_ge(y_out, E * (L + 1))
                    with pe.Fori(0, ROUNDS - 1) as r:
                        with pe.Fori(0, E) as e:
                            n = r * E + e
                            pe.wait_ge(v["in"], 16 * (n + 1))
                            for k in range(KC):
                                ins = pe.transpose(XT[0][:, k * P:(k + 1) * P], xs[:, 0, k * P:(k + 1) * P], ident[:, :])
                            ins.then_inc(v["T"], 1)
                            pe.wait_ge(v["xsT"], n + 1)
                            for k in range(KC):
                                ins = pe.matmul(O[0][:, 0:D], xsT[:, 0, k, :],
                                                w_exp[:, bass.ds(e, 1), k, :].rearrange("p a o -> p (a o)"),
                                                start=(k == 0), stop=(k == KC - 1))
                            ins.then_inc(v["y"], 1)
                    pe.wait_ge(v["yout"], (ROUNDS - 1) * E)

            def project(g):
                pe.wait_ge(xt_out, xt_attn(g) + 2)
                for c in range(KC):
                    n = KC * g + c
                    for w, ready, free in ((0, pg_ready, tg_done), (1, pv_ready, st_done), (2, pq_ready, tq_done)):
                        pe.wait_ge(free, n)
                        for k in range(KC):
                            ins = pe.matmul(PJ[w][:, 0:GT], w_att[:, w, k, c * P:(c + 1) * P],
                                            xaT[:, g, k, :],
                                            start=(k == 0), stop=(k == KC - 1))
                        ins.then_inc(ready, 1)

            def out_project(g):
                pe.wait_ge(ld_done, KC * (g + 1))
                for j in range(J):
                    if j < 2:
                        pe.wait_ge(x2_done, J * g)
                    else:
                        pe.wait_ge(x2_done, J * g + j - 1)
                    for c in range(KC):
                        ins = pe.matmul(O[j % 2][:, 0:D], load[:, c, j * P:(j + 1) * P], w_out[:, c, :],
                                        start=(c == 0), stop=(c == KC - 1))
                    ins.then_inc(o_ready, 1)

            pe.wait_ge(ident_done, 1)
            pe.wait_ge(small_in, 64)
            for k in range(KC):
                pe.transpose(PJ[0][:, k * E:(k + 1) * E], r_nat[:, k * P:(k + 1) * P], ident[0:E, 0:E])
            pe.transpose(PJ[0][:, KC * E:KC * E + 6], vec_rows[:, :], ident[0:6, 0:6]).then_inc(small_T, 1)

            transpose_ffn(0, 0)
            pe.wait_ge(small_ready, 1)
            pe.wait_ge(below_done, 1)
            pe.wait_ge(consts_done, 4)
            logits(0, 0)
            pe.wait_ge(qs_done, 2)
            for c in range(KC):
                for k in range(KC):
                    ins = pe.transpose(PJ[2][:, k * D + c * P:k * D + (c + 1) * P], w_low[:, c, k * P:(k + 1) * P],
                                       ident[:, :])
            ins.then_inc(qsT_full, 1)
            for g in range(1, GROUPS):
                transpose_ffn(0, g)
                ranks(0, g - 1)
                logits(0, g)
            ranks(0, GROUPS - 1)
            counts(0)
            pe.wait_ge(small_ready, 2)
            experts(0)
            overflow(0)

            pe.wait_ge(att_ready, 2)
            pe.wait_ge(w_ready, E)
            pe.wait_ge(y_out, E)
            transpose_mem(0)
            project(0)
            transpose_mem(1)
            for i in range(1, GROUPS - 1):
                out_project(i - 1)
                project(i)
                transpose_ffn(1, i - 1)
                logits(1, i - 1)
                transpose_mem(i + 1)
                ranks(1, i - 1)
            out_project(GROUPS - 2)
            project(GROUPS - 1)
            transpose_ffn(1, GROUPS - 2)
            logits(1, GROUPS - 2)
            ranks(1, GROUPS - 2)
            out_project(GROUPS - 1)
            transpose_ffn(1, GROUPS - 1)
            logits(1, GROUPS - 1)
            ranks(1, GROUPS - 1)
            counts(1)
            pe.wait_ge(x2_done, TILES)
            experts(1)
            overflow(1)


_INS = ["L0_attn_x", "L0_attn_Wv", "L0_attn_Wg", "L0_attn_bg", "L0_attn_Wq", "L0_attn_bq", "L0_attn_Wo",
        "L0_ffn_weight", "L0_ffn_scale", "L0_ffn_expert_masks", "L0_ffn_router_w"]


def kernel(**inputs):
    import concourse.bacc as bacc
    from concourse.bass_utils import run_bass_kernel_spmd

    nc = bacc.Bacc("TRN2", target_bir_lowering=False, num_devices=1)
    arrays, args = {}, []
    for name in _INS:
        a = np.ascontiguousarray(inputs[name])
        arrays[f"in_{name}"] = a
        args.append(nc.dram_tensor(f"in_{name}", a.shape, mybir.dt.from_np(a.dtype), kind="ExternalInput").ap())
    x = arrays["in_L0_attn_x"]
    out = nc.dram_tensor("out_x", x.shape, F32, kind="ExternalOutput").ap()
    macaron_block(nc, *args, out)
    r = run_bass_kernel_spmd(nc, [arrays], core_ids=[0])
    return r.results[0]["out_x"]
```

```python
from contextlib import ExitStack

import numpy as np
import concourse.bass as bass
from concourse import mybir

F32 = mybir.dt.float32
F32R = mybir.dt.float32r
BF16 = mybir.dt.bfloat16
I32 = mybir.dt.int32
U32 = mybir.dt.uint32
U16 = mybir.dt.uint16
ALU = mybir.AluOpType
ACT = mybir.ActivationFunctionType
AX = mybir.AxisListType

P = 128
EPS = 1e-5
DECAY = 0.95
THRESH = 0.5
TILES_PER_GROUP = 4
CHUNK = 4
BODY = 2 * CHUNK
AHEAD = 16


def macaron_block(nc, x, wv, wg, bg, wq, bq, wo, weight, scale, masks, router, out):
    B, S, D = x.shape
    E = masks.shape[0]
    TOKENS = B * S
    TILES = TOKENS // P
    J = TILES_PER_GROUP
    GROUPS = TILES // J
    GT = J * P
    SEQS = GT // S
    KC = D // P
    ROUNDS = TOKENS // P
    SKIP = 1 << 16
    CHUNKS = E // CHUNK
    PAIRS = E // 2
    BP = BODY // 2
    GATE = float(np.float32(np.sqrt(1.0 - DECAY))) ** 2 / 4
    assert D == KC * P and TILES == GROUPS * J and GT == SEQS * S and GT <= 512 and KC == 2
    assert E % BODY == 0 and J * E <= 128 and GROUPS == 4 and 2 * D <= 512 and AHEAD * 2 == E

    x_rows = x.rearrange("b s d -> (b s) d").rearrange("(t p) d -> p t d", p=P)
    out_rows = out.rearrange("b s d -> (b s) d").rearrange("(t p) d -> p t d", p=P)
    mask_rows = masks.rearrange("e o i -> (e o) i").rearrange("(n p) i -> p n i", p=P)

    xs_dram = nc.dram_tensor("rows_by_expert", (E * P, D), F32, kind="Internal").ap()
    ys_dram = nc.dram_tensor("results_by_expert", (E * P, D), F32, kind="Internal").ap()
    xs_tiles = xs_dram.rearrange("(e p) d -> p e d", p=P)
    ys_tiles = ys_dram.rearrange("(e p) d -> p e d", p=P)
    LAST_ROW = E * P - 1

    with ExitStack() as ctx:
        def sb(name, shape, dt=F32):
            return ctx.enter_context(nc.sbuf_tensor(name, shape, dt))

        def psum(name):
            return ctx.enter_context(nc.psum_tensor(name, [P, 512], F32))

        def sem(name):
            return ctx.enter_context(nc.semaphore(name))

        def sems(*names):
            return [sem(name) for name in names]

        w_exp = sb("w_exp", [P, E, KC, D], F32R)
        xs = sb("xs", [P, BODY, D])
        ys = sb("ys", [P, BODY, D])
        xt = sb("xt", [P, TILES, D])
        xf = sb("xf", [P, TILES, D])
        xfT = sb("xfT", [P, KC, GT])
        xa_hi = sb("xa_hi", [P, 2, KC, GT], F32R)
        xa_lo = sb("xa_lo", [P, 2, KC, GT], F32R)
        mask_raw = sb("mask_raw", [P, 2, KC * CHUNK, D])
        xa = mask_raw[:, 0, 0:J, :]
        low_bits = xfT[:, 0, 0:KC * D].bitcast(BF16).rearrange("p (b n) -> p b n", b=2)
        low_sum = sb("low_sum", [P, E])
        low_max = sb("low_max", [P, 1])
        w_hi = sb("w_hi", [P, 4, KC, D], F32R)
        w_lo = sb("w_lo", [P, 4, KC, D], F32R)
        work = sb("work", [P, 4, KC, GT])
        tanh_g, tanh_q, store, mem = (work[:, i] for i in range(4))
        w_raw = work[:, 0:2].rearrange("p a k t -> p (a k t)").rearrange("p (w k d) -> p w k d", w=4, k=KC)
        zeros = work[:, 2:4].rearrange("p a k t -> p (a k t)").rearrange("p (e d) -> p e d", d=D)
        load = sb("load", [P, KC, GT])
        load_hi = sb("load_hi", [P, KC, GT], F32R)
        load_lo = sb("load_lo", [P, KC, GT], F32R)
        xs_hi, xs_lo = load_hi, load_lo
        xs_one = load[:, 0, 0:KC * P].rearrange("p (k c) -> p k c", k=KC)
        w_one = load[:, 1, 0:KC * D].rearrange("p (k o) -> p k o", k=KC)
        w_nat = xs[:, 0:KC, :]
        w_low = xs[:, KC:2 * KC, :]
        w_qT = sb("w_qT", [P, KC, D])
        scale_b = sb("scale_b", [P, D])
        r_nat = sb("r_nat", [E, D])
        rT = sb("rT", [P, KC, E])
        vec_rows = sb("vec_rows", [4, P])
        half_b = sb("half_b", [P, 4])
        ident = sb("ident", [P, P])
        ones_f = sb("ones_f", [P, P])
        below = sb("below", [P, P], BF16)
        ones = sb("ones", [P, P], BF16)
        iota_e = sb("iota_e", [P, E], I32)
        expert = sb("expert", [P, E], BF16)
        prefer = sb("prefer", [P, E])
        decay = sb("decay", [P, S])
        neg_half = sb("neg_half", [P, J])
        NI = 3 * GROUPS
        stats = sb("stats", [P, NI, J, 6])
        mv = sb("mv", [P, NI, J, 2])
        var_eps = sb("var_eps", [P, NI, J])
        rstd = sb("rstd", [P, NI, J])
        nmr = sb("nmr", [P, NI, J])
        top = sb("top", [P, TILES])
        lm = sb("lm", [P, TILES, E])
        cand = sb("cand", [P, J, E])
        best = sb("best", [P, J])
        hot = sb("hot", [P, TILES, E], BF16)
        pos = sb("pos", [P, J, E])
        slot = sb("slot", [P, TILES])
        limit = sb("limit", [P, TILES])
        late = sb("late", [P, TILES])
        early = sb("early", [P, TILES])
        row = sb("row", [P, TILES], U32)
        esum = sb("esum", [P, TILES])
        prob = sb("prob", [P, TILES])
        half_w = sb("half_w", [P, TILES])
        most = sb("most", [P, 2])
        over_f = sb("over_f", [P, 2])
        low_f = sb("low_f", [P, 1])
        flag = sb("flag", [P, 2], I32)

        XT = [psum("XT0"), psum("XT1")]
        PJ = [psum("PG"), psum("PV"), psum("PQ")]
        O = [psum("O0"), psum("O1")]
        RT = psum("RT")
        LG = RT[:, 0:J * E]
        RK = [PJ[2][:, 0:J * E], RT[:, J * E:2 * J * E]]
        CN = RT[:, 2 * J * E:2 * J * E + E]
        LOW = RT[:, 2 * J * E + E:2 * J * E + E + 1]

        x_in = sems(*[f"x_in{g}" for g in range(GROUPS)])
        w_in, r_in, b_in, scale_in, att_in = sems("w_in", "r_in", "b_in", "scale_in", "att_in")
        mask_in = sems("mask_in0", "mask_in1")
        zero_src, zeroed = sems("zero_src", "zeroed")
        iota_done, ident_done, ones_f_done, below_done = sems("iota_done", "ident_done", "ones_f_done", "below_done")
        ones_done, consts_done, neg_half_done = sems("ones_done", "consts_done", "neg_half_done")
        small_T, small_ready, low_done, quant_done = sems("small_T", "small_ready", "low_done", "quant_done")
        qT_full, qT_ready, wo_scaled, w_hi_done, w_lo_done = sems("qT_full", "qT_ready", "wo_scaled", "w_hi_done",
                                                                  "w_lo_done")
        mask_T, mask_tested, w_ready = sems("mask_T", "mask_tested", "w_ready")
        ln = {k: {s: sem(f"ln{k}_{s}") for s in ("stats", "mv", "var", "rstd", "nmr", "xn")} for k in "FA"}
        xt_full, xt_out, xt_lo = sems("xt_full", "xt_out", "xt_lo")
        lg_ready, top_done, lg_read, cand_done = sems("lg_ready", "top_done", "lg_read", "cand_done")
        best_done, hot_done, rk_ready, pos_done = sems("best_done", "hot_done", "rk_ready", "pos_done")
        slot_done, limit_done, late_done, row_done = sems("slot_done", "limit_done", "late_done", "row_done")
        scattered, cn_ready, most_done, over_done = sems("scattered", "cn_ready", "most_done", "over_done")
        lowmax_done, low_ready, low_f_done, flag_done = sems("lowmax_done", "low_ready", "low_f_done", "flag_done")
        exp_done, esum_done, prob_done, half_done = sems("exp_done", "esum_done", "prob_done", "half_done")
        xs_in = sems("xs_in0", "xs_in1")
        y_full, y_out = sems("y_full", "y_out")
        ys_written = sems("ys_written0", "ys_written1")
        gathered = sems(*[f"gathered{g}" for g in range(GROUPS)])
        x1_done, x2_done, x3_done, out_written = sems("x1_done", "x2_done", "x3_done", "out_written")
        pg_ready, pv_ready, pq_ready = sems("pg_ready", "pv_ready", "pq_ready")
        tg_done, tq_done, st_done, mem_done = sems("tg_done", "tq_done", "st_done", "mem_done")
        ld_done, ld_hi_done, ld_lo_done, o_ready = sems("ld_done", "ld_hi_done", "ld_lo_done", "o_ready")
        rd = [{s: sem(f"rounds{L}_{s}") for s in ("step", "cur", "edge", "row", "scat", "gath", "free", "rows", "mask",
                                                  "T", "xT", "w", "y", "yout", "st")} for L in range(2)]

        F, A = [("F", False)] * 2, [("A", True)] * 2
        uses = GROUPS * F + [("E", True)] * PAIRS + A
        XT_EXP = [GROUPS * 2, 0]
        XT_ATT, XT_FFN = [XT_EXP[0] + PAIRS], [[2 * g for g in range(GROUPS)], []]
        for i in range(GROUPS + 2):
            if i + 1 < GROUPS:
                XT_ATT.append(len(uses))
                uses = uses + A
            if i >= 2:
                XT_FFN[1].append(len(uses))
                uses = uses + F
        XT_EXP[1] = len(uses)
        uses = uses + [("E", True)] * PAIRS

        def lo_before(u):
            return sum(lo for _, lo in uses[:u])

        LO_EXP = [lo_before(XT_EXP[L]) for L in range(2)]
        Y_CREDIT, W_CREDIT, M_CREDIT, YS_CREDIT = 2, 2, 2, 16

        def tiles(g):
            return slice(g * J, (g + 1) * J)

        def rounds_needed(eng, L):
            eng.wait_ge(flag_done, L + 1)
            return eng.value_load(flag[0:1, L:L + 1], min_val=0, max_val=1) > 0

        block = ctx.enter_context(nc.Block())

        @block.sync
        def _(sp):
            for g in range(GROUPS):
                sp.dma_start(xt[:, tiles(g), :], x_rows[:, tiles(g), :]).then_inc(x_in[g], 16)
                if g == 0:
                    sp.dma_start(r_nat[:, :], router).then_inc(r_in, 16)
            sp.dma_start(w_nat, weight.rearrange("(c p) i -> p c i", p=P)).then_inc(w_in, 16)
            sp.wait_ge(zero_src, 1)
            for c in range(E // BODY):
                sp.dma_start(xs_tiles[:, c * BODY:(c + 1) * BODY, :], zeros).then_inc(zeroed, 16)

            def load_masks(c, b):
                sp.dma_start(mask_raw[:, b], mask_rows[:, c * KC * CHUNK:(c + 1) * KC * CHUNK, :]).then_inc(mask_in[b], 16)

            for c in range(2):
                load_masks(c, c)
            for k, v in enumerate((bg, bq)):
                sp.dma_start(vec_rows[2 * k:2 * k + 2, :], v.rearrange("(c p) -> c p", p=P)).then_inc(b_in, 16)
            sp.dma_start(scale_b[:, :], scale.partition_broadcast(P)).then_inc(scale_in, 16)
            for k, w in enumerate((wg, wv, wq, wo)):
                sp.dma_start(w_raw[:, k], w.rearrange("(c p) m -> p c m", p=P)).then_inc(att_in, 16)

            def next_masks(c):
                sp.wait_ge(mask_T, CHUNK * (c - 1))
                sp.wait_ge(mask_tested, M_CREDIT + CHUNK * (c - 1))
                load_masks(c, c % 2)

            def load_rows(c, b):
                sp.dma_start(xs[:, b * CHUNK:(b + 1) * CHUNK, :],
                             xs_tiles[:, bass.ds(c * CHUNK, CHUNK), :]).then_inc(xs_in[b], 16)

            def next_rows(L, c, b):
                sp.wait_ge(xt_full, XT_EXP[L] + CHUNK // 2 * (c - 1))
                load_rows(c, b)

            def store_results(L, c, b):
                sp.wait_ge(y_out, Y_CREDIT + PAIRS * L + CHUNK // 2 * (c + 1))
                sp.dma_start(ys_tiles[:, bass.ds(c * CHUNK, CHUNK), :],
                             ys[:, b * CHUNK:(b + 1) * CHUNK, :]).then_inc(ys_written[b], 16)

            for L in range(2):
                if L == 0:
                    for c in range(2, AHEAD // CHUNK + 2):
                        next_masks(c)
                    sp.wait_ge(zeroed, 16 * (E // BODY))
                    sp.wait_ge(qT_full, 1)
                sp.wait_ge(scattered, 16 * TILES * (L + 1))
                load_rows(0, 0)
                load_rows(1, 1)
                if L == 0:
                    for c in range(2):
                        next_rows(L, c + 2, c)
                        next_masks(AHEAD // CHUNK + 2 + c)
                        store_results(L, c, c)
                with sp.Fori(1 - L, CHUNKS // 2 - 1) as i:
                    for b in range(2):
                        next_rows(L, 2 * i + b + 2, b)
                        store_results(L, 2 * i + b, b)
                for c in range(CHUNKS - 2, CHUNKS):
                    store_results(L, c, c % 2)

                with sp.If(rounds_needed(sp, L)):
                    v = rd[L]
                    for b in range(2):
                        sp.wait_ge(ys_written[b], YS_CREDIT + 16 * CHUNKS // 2 * (L + 1))
                    with sp.Fori(0, ROUNDS) as r:
                        with sp.Fori(0, E) as e:
                            n = r * E + e
                            sp.wait_ge(v["scat"], 16 * TILES * (r + 1))
                            sp.dma_start(xs[:, 0:1, :], xs_tiles[:, bass.ds(e, 1), :]).then_inc(v["rows"], 16)
                            sp.dma_start(mask_raw[:, 0, 0:KC, :], mask_rows[:, bass.ds(e * KC, KC), :]
                                         ).then_inc(v["mask"], 16)
                            sp.wait_ge(v["yout"], n + 1)
                            sp.dma_start(ys_tiles[:, bass.ds(e, 1), :], ys[:, 0:1, :]).then_inc(v["st"], 16)

            for g in range(GROUPS):
                sp.wait_ge(x3_done, J * (g + 1))
                sp.dma_start(out_rows[:, tiles(g), :], xt[:, tiles(g), :]).then_inc(out_written, 16)
            sp.wait_ge(out_written, 16 * GROUPS)

        @block.gpsimd
        def _(pool):
            pool.memset(ones_f[:, :], 1.0).then_inc(ones_f_done, 1)
            pool.memset(neg_half[:, :], -0.5).then_inc(neg_half_done, 1)
            pool.wait_ge(ones_f_done, 1)
            pool.affine_select(out=ident[:, :], in_=ones_f[:, :], pattern=[[1, P]], compare_op=ALU.is_equal,
                               fill=0.0, base=0, channel_multiplier=-1).then_inc(ident_done, 1)
            pool.iota(iota_e[:, :], pattern=[[1, E]], base=0, channel_multiplier=0).then_inc(iota_done, 1)
            pool.wait_ge(ones_done, 1)
            pool.affine_select(out=below[:, :], in_=ones[:, :], pattern=[[1, P]], compare_op=ALU.is_gt,
                               fill=0.0, base=0, channel_multiplier=-1).then_inc(below_done, 1)
            for b in range(2):
                pool.sem_inc(ys_written[b], YS_CREDIT)
            pool.wait_ge(neg_half_done, 1)

            def inv_std(kind, n, q):
                pool.wait_ge(ln[kind]["var"], n + 1)
                pool.tensor_tensor(rstd[:, q, :], var_eps[:, q, :], neg_half[:, :], ALU.pow).then_inc(ln[kind]["rstd"], 1)

            def scatter_tile(t, done):
                pool.indirect_dma_start(xs_dram, bass.IndirectOffsetOnAxis(ap=row[:, t:t + 1], axis=0), xf[:, t, :],
                                        None, bounds_check=LAST_ROW, oob_is_err=False).then_inc(done, 16)

            def gather_tile(t, done):
                pool.indirect_dma_start(xf[:, t, :], None, ys_dram,
                                        bass.IndirectOffsetOnAxis(ap=row[:, t:t + 1], axis=0),
                                        bounds_check=LAST_ROW, oob_is_err=False).then_inc(done, 16)

            def scatter(L, g):
                n = L * GROUPS + g
                pool.wait_ge(row_done, n + 1)
                pool.wait_ge(ln["F"]["xn"], J * (n + 1))
                for t in range(g * J, (g + 1) * J):
                    scatter_tile(t, scattered)

            def gather(L):
                pool.wait_ge(scattered, 16 * TILES * (L + 1))
                with pool.If(rounds_needed(pool, L)):
                    v = rd[L]
                    pool.sem_inc(v["free"], 1)
                    with pool.Fori(0, ROUNDS) as r:
                        pool.wait_ge(v["row"], r + 1)
                        pool.sem_inc(v["step"], 1)
                        for t in range(TILES):
                            scatter_tile(t, v["scat"])
                        pool.wait_ge(v["st"], 16 * E * (r + 1))
                        pool.sem_inc(v["step"], 1)
                        for t in range(TILES):
                            gather_tile(t, v["gath"])
                        pool.wait_ge(v["gath"], 16 * TILES * (r + 1))
                        pool.sem_inc(v["free"], 1)
                for b in range(2):
                    pool.wait_ge(ys_written[b], YS_CREDIT + 16 * CHUNKS // 2 * (L + 1))
                for t in range(TILES):
                    gather_tile(t, gathered[t // J])

            def split_load(g):
                for c in range(KC):
                    pool.wait_ge(ld_hi_done, KC * g + c + 1)
                    if g > 0:
                        pool.wait_ge(o_ready, 2 * g)
                    pool.tensor_tensor(load_lo[:, c, :], load[:, c, :], load_hi[:, c, :], ALU.subtract
                                       ).then_inc(ld_lo_done, 1)

            inv_std("F", 0, 0)
            inv_std("F", 1, 1)
            pool.memset(zeros, 0.0).then_inc(zero_src, 1)
            inv_std("F", 2, 2)
            inv_std("F", 3, 3)
            pool.wait_ge(zeroed, 16 * (E // BODY))
            for g in range(GROUPS):
                scatter(0, g)
            gather(0)
            QA = 2 * GROUPS
            inv_std("A", 0, QA)
            inv_std("A", 1, QA + 1)
            for i in range(GROUPS + 3):
                if 0 <= i - 1 < GROUPS:
                    split_load(i - 1)
                if i + 2 < GROUPS:
                    inv_std("A", i + 2, QA + i + 2)
                if 0 <= i - 1 < GROUPS:
                    inv_std("F", GROUPS + i - 1, GROUPS + i - 1)
                if 0 <= i - 3 < GROUPS:
                    scatter(1, i - 3)
            gather(1)

        @block.scalar
        def _(act):
            def normalise(kind, n, q, g, dst):
                act.wait_ge(ln[kind]["nmr"], n + 1)
                for j in range(J):
                    act.activation(dst[:, j, :], xt[:, g * J + j, :], ACT.Identity, bias=nmr[:, q, j:j + 1],
                                   scale=rstd[:, q, j:j + 1]).then_inc(ln[kind]["xn"], 1)

            def normalise_ffn(L, g):
                n = L * GROUPS + g
                if L == 1:
                    act.wait_ge(x1_done, J * (g + 1))
                normalise("F", n, n, g, xf[:, tiles(g), :])

            def normalise_mem(g):
                if g > 0:
                    act.wait_ge(xt_full, XT_ATT[g - 1] + 2)
                normalise("A", g, 2 * GROUPS + g, g, xa)

            def copy_T(u, dst):
                for h in range(2):
                    act.wait_ge(xt_full, u + h + 1)
                    act.copy(dst[:, :, h * 2 * P:(h + 1) * 2 * P].rearrange("p k (j c) -> p k j c", j=2),
                             XT[h][:, :].rearrange("p (j k c) -> p k j c", j=2, k=KC)).then_inc(xt_out, 1)

            def copy_T_ffn(L, g):
                n = L * GROUPS + g
                if n > 0:
                    act.wait_ge(lg_ready, n)
                copy_T(XT_FFN[L][g], xfT)

            def copy_T_mem(g):
                if g > 1:
                    act.wait_ge(pq_ready, KC * (g - 1))
                copy_T(XT_ATT[g], xa_hi[:, g % 2])

            def exponentials(L):
                act.wait_ge(lg_read, (J + 1) * GROUPS * (L + 1))
                act.activation(lm[:, :, :], lm[:, :, :], ACT.Exp).then_inc(exp_done, 1)

            def test_mask(e, slot_):
                act.wait_ge(mask_tested, e - 1 + M_CREDIT)
                act.activation(low_bits[:, slot_ % 2], mask_raw[:, slot_ // CHUNK, KC * (slot_ % CHUNK):KC * (slot_ % CHUNK + 1), :]
                               .rearrange("p c i -> p (c i)").bitcast(U16).rearrange("p (n h) -> p n h", h=2)[:, :, 0],
                               ACT.Copy, accum_out=low_sum[:, bass.ds(e, 1)]).then_inc(mask_tested, 1)

            def test_masks(i):
                for s in range(2):
                    act.wait_ge(mask_in[s], 16 * (i + 1))
                    for m in range(CHUNK):
                        test_mask(BODY * i + CHUNK * s + m, CHUNK * s + m)

            def round_rows(L, q, b):
                act.wait_ge(xt_full, XT_EXP[L] + q + 1)
                act.wait_ge(y_full, PAIRS * L + q - 1 + Y_CREDIT)
                act.copy(xs_hi[:, b, :], XT[b][:, :]).then_inc(xt_out, 1)

            def experts(L):
                if L == 0:
                    with act.Fori(0, AHEAD // BODY) as i:
                        test_masks(i)
                    with act.Fori(AHEAD // BODY, E // BODY) as i:
                        for m in range(BP):
                            round_rows(L, BP * i + m - AHEAD // 2, m % 2)
                            if m % 2 == 0:
                                act.wait_ge(mask_in[m // 2], 16 * (i + 1))
                            for k in range(2):
                                test_mask(BODY * i + 2 * m + k, 2 * m + k)
                with act.Fori((1 - L) * AHEAD // BODY, E // BODY) as i:
                    for m in range(BP):
                        round_rows(L, BP * i + m, m % 2)

            def rounds(L):
                with act.If(rounds_needed(act, L)):
                    v = rd[L]
                    with act.Fori(0, ROUNDS * E) as n:
                        act.wait_ge(v["T"], n + 1)
                        act.copy(xs_one[:, :, :], XT[0][:, 0:KC * P].rearrange("p (k c) -> p k c", k=KC)).then_inc(v["xT"], 1)

            def tanhs(g, c):
                n = KC * g + c
                act.wait_ge(pg_ready, n + 1)
                if g > 0:
                    act.wait_ge(st_done, KC * g)
                    act.wait_ge(ld_done, KC * g)
                act.activation(tanh_g[:, c, :], PJ[0][:, 0:GT], ACT.Tanh, bias=half_b[:, c:c + 1],
                               scale=0.5).then_inc(tg_done, 1)
                act.wait_ge(pq_ready, n + 1)
                act.activation(tanh_q[:, c, :], PJ[2][:, 0:GT], ACT.Tanh, bias=half_b[:, 2 + c:3 + c],
                               scale=0.5).then_inc(tq_done, 1)

            def round_load(g, c):
                n = KC * g + c
                act.wait_ge(ld_done, n + 1)
                if g > 0:
                    act.wait_ge(o_ready, 2 * g)
                act.copy(load_hi[:, c, :], load[:, c, :]).then_inc(ld_hi_done, 1)

            act.sem_inc(mask_tested, M_CREDIT)
            normalise_ffn(0, 0)
            normalise_ffn(0, 1)
            copy_T_ffn(0, 0)
            normalise_ffn(0, 2)
            copy_T_ffn(0, 1)
            normalise_ffn(0, 3)
            copy_T_ffn(0, 2)
            copy_T_ffn(0, 3)
            exponentials(0)
            act.wait_ge(att_in, 64)
            act.wait_ge(wo_scaled, 1)
            act.copy(w_hi[:, :, :, :], w_raw).then_inc(w_hi_done, 1)
            experts(0)
            rounds(0)

            normalise_mem(0)
            copy_T_mem(0)
            for i in range(GROUPS + 2):
                if 0 <= i - 1 < GROUPS:
                    for c in range(KC):
                        round_load(i - 1, c)
                if i + 1 < GROUPS:
                    normalise_mem(i + 1)
                if i < GROUPS:
                    tanhs(i, 0)
                if i + 1 < GROUPS:
                    copy_T_mem(i + 1)
                if i >= 2:
                    normalise_ffn(1, i - 2)
                if i < GROUPS:
                    tanhs(i, 1)
                if i >= 2:
                    copy_T_ffn(1, i - 2)
            exponentials(1)
            experts(1)
            rounds(1)

        @block.vector
        def _(dve):
            def norm_stats(kind, n, q, g):
                s = ln[kind]
                for j in range(J):
                    dve.bn_stats(stats[:, q, j, :], xt[:, g * J + j, :]).then_inc(s["stats"], 1)
                for j in range(J):
                    dve.wait_ge(s["stats"], J * n + j + 1)
                    dve.bn_aggr(mv[:, q, j, :], stats[:, q, j, :]).then_inc(s["mv"], 1)
                dve.wait_ge(s["mv"], J * (n + 1))
                dve.tensor_scalar(var_eps[:, q, :], mv[:, q, :, 1], EPS, None, ALU.add).then_inc(s["var"], 1)

            def norm_bias(kind, n, q):
                dve.wait_ge(ln[kind]["rstd"], n + 1)
                dve.scalar_tensor_tensor(out=nmr[:, q, :], in0=mv[:, q, :, 0], scalar=-1.0, in1=rstd[:, q, :],
                                         op0=ALU.mult, op1=ALU.mult).then_inc(ln[kind]["nmr"], 1)

            def choose(L, g):
                n = L * GROUPS + g
                lg = LG.rearrange("p (j e) -> p j e", j=J)
                dve.wait_ge(lg_ready, n + 1)
                dve.tensor_reduce(top[:, tiles(g)], lg, AX.X, ALU.max).then_inc(top_done, 1)
                dve.wait_ge(top_done, n + 1)
                for j in range(J):
                    dve.scalar_tensor_tensor(out=cand[:, j, :], in0=lg[:, j, :], scalar=top[:, g * J + j:g * J + j + 1],
                                             in1=prefer[:, :], op0=ALU.is_equal, op1=ALU.mult).then_inc(lg_read, 1)
                dve.tensor_tensor(lm[:, tiles(g), :], lg, top[:, tiles(g)].unsqueeze(2).to_broadcast([P, J, E]),
                                  ALU.subtract).then_inc(lg_read, 1)
                dve.wait_ge(lg_read, (J + 1) * n + J)
                dve.tensor_reduce(best[:, :], cand[:, :, :], AX.X, ALU.max).then_inc(best_done, 1)
                dve.wait_ge(best_done, n + 1)
                dve.tensor_tensor(hot[:, tiles(g), :], cand[:, :, :],
                                  best[:, :].unsqueeze(2).to_broadcast([P, J, E]), ALU.is_equal).then_inc(hot_done, 1)
                dve.tensor_scalar(limit[:, tiles(g)], best[:, :], -float(P), float((E + 1) * P), ALU.mult,
                                  ALU.add).then_inc(limit_done, 1)

            def number(L, g):
                n = L * GROUPS + g
                dve.wait_ge(rk_ready, n + 1)
                dve.tensor_tensor(pos[:, :, :], hot[:, tiles(g), :], RK[L].rearrange("p (j e) -> p j e", j=J),
                                  ALU.mult).then_inc(pos_done, 1)
                dve.wait_ge(pos_done, n + 1)
                dve.tensor_reduce(slot[:, tiles(g)], pos[:, :, :], AX.X, ALU.add).then_inc(slot_done, 1)
                dve.wait_ge(slot_done, n + 1)
                dve.wait_ge(limit_done, n + 1)
                dve.tensor_tensor(late[:, tiles(g)], slot[:, tiles(g)], limit[:, tiles(g)],
                                  ALU.is_ge).then_inc(late_done, 1)
                dve.wait_ge(late_done, n + 1)
                dve.scalar_tensor_tensor(out=row[:, tiles(g)], in0=late[:, tiles(g)], scalar=float(SKIP),
                                         in1=slot[:, tiles(g)], op0=ALU.mult, op1=ALU.add).then_inc(row_done, 1)

            def too_many(L):
                dve.wait_ge(cn_ready, L + 1)
                dve.tensor_reduce(most[:, L:L + 1], CN, AX.X, ALU.max).then_inc(most_done, 1)
                dve.wait_ge(most_done, L + 1)
                dve.tensor_scalar(over_f[:, L:L + 1], most[:, L:L + 1], float(P), None, ALU.is_gt).then_inc(over_done, 1)

            def masks_have_low_bits():
                dve.wait_ge(mask_tested, M_CREDIT + E)
                dve.tensor_reduce(low_max[:, :], low_sum[:, :], AX.X, ALU.max).then_inc(lowmax_done, 1)
                dve.wait_ge(low_ready, 1)
                dve.tensor_scalar(low_f[:, :], LOW, 0.0, None, ALU.is_gt).then_inc(low_f_done, 1)

            def set_flag(L):
                dve.wait_ge(over_done, L + 1)
                dve.wait_ge(low_f_done, 1)
                dve.tensor_tensor(flag[:, L:L + 1], over_f[:, L:L + 1], low_f[:, :], ALU.max).then_inc(flag_done, 1)

            def rounds(L):
                with dve.If(rounds_needed(dve, L)):
                    v = rd[L]
                    with dve.Fori(0, ROUNDS) as r:
                        dve.tensor_tensor(late[:, :], slot[:, :], limit[:, :], ALU.is_ge).then_inc(v["edge"], 1)
                        dve.scalar_tensor_tensor(out=early[:, :], in0=slot[:, :], scalar=float(P), in1=limit[:, :],
                                                 op0=ALU.add, op1=ALU.is_lt).then_inc(v["edge"], 1)
                        dve.wait_ge(v["edge"], 3 * r + 2)
                        dve.tensor_tensor(late[:, :], late[:, :], early[:, :], ALU.add).then_inc(v["edge"], 1)
                        dve.wait_ge(v["edge"], 3 * r + 3)
                        dve.wait_ge(v["free"], r + 1)
                        dve.scalar_tensor_tensor(out=row[:, :], in0=late[:, :], scalar=float(SKIP), in1=slot[:, :],
                                                 op0=ALU.mult, op1=ALU.add).then_inc(v["row"], 1)
                        dve.wait_ge(v["row"], r + 1)
                        dve.tensor_scalar(slot[:, :], slot[:, :], -float(P), None, ALU.add).then_inc(v["cur"], 1)
                        with dve.Fori(0, E) as e:
                            n = r * E + e
                            dve.wait_ge(v["T"], n + 1)
                            dve.tensor_tensor(w_one[:, :, :], PJ[0][:, :].rearrange("p (k o) -> p k o", k=KC),
                                              w_qT[:, :, :], ALU.mult).then_inc(v["w"], 1)
                            dve.wait_ge(v["y"], n + 1)
                            dve.tensor_tensor(ys[:, 0, :], O[0][:, 0:D], scale_b[:, :], ALU.mult).then_inc(v["yout"], 1)
                        dve.wait_ge(v["cur"], r + 1)
                    dve.wait_ge(v["free"], ROUNDS + 1)

            def top_weights(L):
                dve.wait_ge(exp_done, L + 1)
                dve.tensor_reduce(esum[:, :], lm[:, :, :], AX.X, ALU.add).then_inc(esum_done, 1)
                dve.wait_ge(esum_done, L + 1)
                dve.reciprocal(prob[:, :], esum[:, :]).then_inc(prob_done, 1)
                dve.wait_ge(prob_done, L + 1)
                dve.tensor_scalar(half_w[:, :], prob[:, :], 0.5, None, ALU.mult).then_inc(half_done, 1)

            def build_weight(e, b):
                dve.wait_ge(mask_T, e + 1)
                dve.tensor_tensor(w_exp[:, bass.ds(e, 1), :, :].rearrange("p a k o -> p (a k) o"),
                                  PJ[b][:, :].rearrange("p (k o) -> p k o", k=KC), w_qT[:, :, :],
                                  ALU.mult).then_inc(w_ready, 1)

            def low_rows(L, q, b):
                dve.wait_ge(xt_out, XT_EXP[L] + q + 1)
                dve.tensor_tensor(xs_lo[:, b, :], XT[b][:, :],
                                  xs_hi[:, b, :], ALU.subtract).then_inc(xt_lo, 1)

            def scale_results(L, q, m):
                dve.wait_ge(y_full, Y_CREDIT + PAIRS * L + q + 1)
                dve.tensor_tensor(ys[:, 2 * m:2 * m + 2, :], O[m % 2][:, :].rearrange("p (e d) -> p e d", e=2),
                                  scale_b[:, :].unsqueeze(1).to_broadcast([P, 2, D]), ALU.mult).then_inc(y_out, 1)

            def expert_turn(L, i, masks, last=False):
                for m in range(BP):
                    q = BP * i + m
                    if not (last and m == BP - 1):
                        low_rows(L, q + 1, (m + 1) % 2)
                    if masks:
                        for k in range(2):
                            build_weight(AHEAD + 2 * q + k, k)
                    if m % 2 == 0:
                        dve.wait_ge(ys_written[m // 2], YS_CREDIT + 16 * (CHUNKS // 2 * L + i))
                    scale_results(L, q, m)

            def experts(L):
                low_rows(L, 0, 0)
                if L == 0:
                    with dve.Fori(0, AHEAD // BODY) as i:
                        expert_turn(L, i, True)
                with dve.Fori((1 - L) * AHEAD // BODY, E // BODY - 1) as i:
                    expert_turn(L, i, False)
                expert_turn(L, E // BODY - 1, False, last=True)

            def add_ffn(L, g, done):
                dve.wait_ge(gathered[g], 16 * J * (L + 1))
                dve.wait_ge(half_done, L + 1)
                for j in range(J):
                    t = g * J + j
                    dve.scalar_tensor_tensor(out=xt[:, t, :], in0=xf[:, t, :], scalar=half_w[:, t:t + 1],
                                             in1=xt[:, t, :], op0=ALU.mult, op1=ALU.add).then_inc(done, 1)

            def add_and_norm_mem(g):
                add_ffn(0, g, x1_done)
                dve.wait_ge(x1_done, J * (g + 1))
                norm_stats("A", g, 2 * GROUPS + g, g)

            def low_mem(g):
                for h in range(2):
                    c = slice(h * 2 * P, (h + 1) * 2 * P)
                    dve.wait_ge(xt_out, XT_ATT[g] + h + 1)
                    dve.tensor_tensor(xa_lo[:, g % 2, :, c].rearrange("p k (j c) -> p k j c", j=2),
                                      XT[h][:, :].rearrange("p (j k c) -> p k j c", j=2, k=KC),
                                      xa_hi[:, g % 2, :, c].rearrange("p k (j c) -> p k j c", j=2),
                                      ALU.subtract).then_inc(xt_lo, 1)

            def memory(g, c):
                n = KC * g + c
                dve.wait_ge(tg_done, n + 1)
                dve.wait_ge(pv_ready, n + 1)
                dve.scalar_tensor_tensor(out=store[:, c, :], in0=tanh_g[:, c, :], scalar=1.0,
                                         in1=PJ[1][:, 0:GT], op0=ALU.add, op1=ALU.mult).then_inc(st_done, 1)
                dve.wait_ge(st_done, n + 1)
                for h in range(SEQS):
                    s = slice(h * S, (h + 1) * S)
                    dve.tensor_tensor_scan(mem[:, c, s], decay[:, :], store[:, c, s], 0.0, ALU.mult,
                                           ALU.add).then_inc(mem_done, 1)
                dve.wait_ge(tq_done, n + 1)
                dve.wait_ge(mem_done, SEQS * (n + 1))
                if g > 0:
                    dve.wait_ge(ld_lo_done, KC * g)
                dve.scalar_tensor_tensor(out=load[:, c, :], in0=tanh_q[:, c, :], scalar=1.0, in1=mem[:, c, :],
                                         op0=ALU.add, op1=ALU.mult).then_inc(ld_done, 1)

            def add_mem_and_norm(g):
                for h in range(2):
                    t = slice(g * J + 2 * h, g * J + 2 * h + 2)
                    dve.wait_ge(o_ready, 2 * g + h + 1)
                    dve.tensor_tensor(xt[:, t, :], xt[:, t, :], O[h][:, :].rearrange("p (j d) -> p j d", j=2),
                                      ALU.add).then_inc(x2_done, 1)
                dve.wait_ge(x2_done, 2 * (g + 1))
                norm_stats("F", GROUPS + g, GROUPS + g, g)

            dve.memset(ones[:, :], 1.0).then_inc(ones_done, 1)
            dve.memset(decay[:, :], DECAY).then_inc(consts_done, 1)
            dve.wait_ge(iota_done, 1)
            dve.tensor_copy(expert[:, :], iota_e[:, :]).then_inc(consts_done, 1)
            dve.tensor_scalar(prefer[:, :], iota_e[:, :], -1.0, float(E), ALU.mult, ALU.add).then_inc(consts_done, 1)
            dve.sem_inc(w_ready, W_CREDIT)
            dve.sem_inc(y_out, Y_CREDIT)

            dve.wait_ge(x_in[0], 16)
            norm_stats("F", 0, 0, 0)
            dve.wait_ge(small_T, 1)
            dve.tensor_copy(rT[:, :, :], PJ[0][:, 0:KC * E].rearrange("p (k e) -> p k e", k=KC)).then_inc(small_ready, 1)
            dve.wait_ge(x_in[1], 16)
            norm_stats("F", 1, 1, 1)
            norm_bias("F", 0, 0)
            dve.wait_ge(x_in[2], 16)
            norm_stats("F", 2, 2, 2)
            norm_bias("F", 1, 1)
            dve.wait_ge(consts_done, 3)
            choose(0, 0)
            norm_bias("F", 2, 2)
            dve.wait_ge(x_in[3], 16)
            norm_stats("F", 3, 3, 3)
            number(0, 0)
            choose(0, 1)
            norm_bias("F", 3, 3)
            dve.wait_ge(w_in, 16)
            dve.tensor_scalar(w_low, w_nat, -THRESH / 2, None, ALU.is_lt).then_inc(low_done, 1)
            number(0, 1)
            choose(0, 2)
            dve.wait_ge(low_done, 1)
            dve.scalar_tensor_tensor(out=w_low, in0=w_nat, scalar=THRESH / 2, in1=w_low, op0=ALU.is_gt,
                                     op1=ALU.subtract).then_inc(quant_done, 1)
            number(0, 2)
            choose(0, 3)
            number(0, 3)
            too_many(0)
            dve.wait_ge(qT_full, 1)
            dve.tensor_copy(w_qT[:, :, :], PJ[0][:, :].rearrange("p (k o) -> p k o", k=KC)).then_inc(qT_ready, 1)
            dve.wait_ge(small_T, 2)
            dve.tensor_scalar(half_b[:, :], PJ[1][:, 0:4], 0.5, None, ALU.mult).then_inc(small_ready, 1)
            dve.wait_ge(att_in, 64)
            dve.tensor_scalar(w_raw[:, 3], w_raw[:, 3], GATE, None, ALU.mult).then_inc(wo_scaled, 1)
            dve.wait_ge(qT_ready, 1)
            with dve.Fori(0, AHEAD // 2) as i:
                for b in range(2):
                    build_weight(2 * i + b, b)
            dve.wait_ge(w_hi_done, 1)
            dve.tensor_tensor(w_lo[:, :, :, :], w_raw, w_hi[:, :, :, :], ALU.subtract).then_inc(w_lo_done, 1)
            dve.wait_ge(scale_in, 16)
            experts(0)
            masks_have_low_bits()
            set_flag(0)
            top_weights(0)
            rounds(0)

            add_and_norm_mem(0)
            add_and_norm_mem(1)
            norm_bias("A", 0, 2 * GROUPS)
            low_mem(0)
            norm_bias("A", 1, 2 * GROUPS + 1)
            for i in range(GROUPS + 3):
                if i < GROUPS:
                    memory(i, 0)
                if i + 1 < GROUPS:
                    low_mem(i + 1)
                if 0 <= i - 3 < GROUPS:
                    number(1, i - 3)
                if i < GROUPS:
                    memory(i, 1)
                if i + 2 < GROUPS:
                    add_and_norm_mem(i + 2)
                if 0 <= i - 1 < GROUPS:
                    add_mem_and_norm(i - 1)
                if i + 2 < GROUPS:
                    norm_bias("A", i + 2, 2 * GROUPS + i + 2)
                if 0 <= i - 1 < GROUPS:
                    norm_bias("F", GROUPS + i - 1, GROUPS + i - 1)
                if 0 <= i - 2 < GROUPS:
                    choose(1, i - 2)
            too_many(1)
            set_flag(1)
            top_weights(1)
            experts(1)
            rounds(1)
            for g in range(GROUPS):
                add_ffn(1, g, x3_done)

        @block.tensor
        def _(pe):
            def transpose_group(kind, n, u, src):
                for h in range(2):
                    if u + h > 1:
                        pe.wait_ge(xt_out, u + h - 1)
                        if lo_before(u + h - 1) > 0:
                            pe.wait_ge(xt_lo, lo_before(u + h - 1))
                    for j in range(2):
                        pe.wait_ge(ln[kind]["xn"], J * n + 2 * h + j + 1)
                        for k in range(KC):
                            at = (j * KC + k) * P
                            ins = pe.transpose(XT[h][:, at:at + P], src[:, 2 * h + j, k * P:(k + 1) * P], ident[:, :])
                    ins.then_inc(xt_full, 1)

            def transpose_mem(g):
                transpose_group("A", g, XT_ATT[g], xa)

            def transpose_ffn(L, g):
                transpose_group("F", L * GROUPS + g, XT_FFN[L][g], xf[:, tiles(g), :])

            def logits(L, g):
                n = L * GROUPS + g
                if n > 0:
                    pe.wait_ge(lg_read, (J + 1) * n)
                if L == 1:
                    pe.wait_ge(low_f_done, 1)
                    pe.wait_ge(pos_done, n)
                for j in range(J):
                    pe.wait_ge(xt_out, XT_FFN[L][g] + j // 2 + 1)
                    for k in range(KC):
                        ins = pe.matmul(LG[:, j * E:(j + 1) * E], xfT[:, k, j * P:(j + 1) * P], rT[:, k, :],
                                        start=(k == 0), stop=(k == KC - 1))
                ins.then_inc(lg_ready, 1)

            def ranks(L, g):
                n = L * GROUPS + g
                pe.wait_ge(hot_done, n + 1)
                if L == 1:
                    pe.wait_ge(lg_read, (J + 1) * (n + 1))
                elif n > 0:
                    pe.wait_ge(pos_done, n)
                rk = RK[L].rearrange("p (j e) -> p j e", j=J)
                pe.matmul(rk, below[:, :], hot[:, tiles(g), :], start=True, stop=False)
                for j in range(J - 1):
                    pe.matmul(rk[:, j + 1:J, :], ones[:, :],
                              hot[:, g * J + j:g * J + j + 1, :].to_broadcast([P, J - 1 - j, E]), start=False, stop=False)
                for t in range(g * J):
                    pe.matmul(rk, ones[:, :], hot[:, t:t + 1, :].to_broadcast([P, J, E]), start=False, stop=False)
                pe.matmul(rk, ones[:, :], expert[:, :].unsqueeze(1).to_broadcast([P, J, E]),
                          start=False, stop=True).then_inc(rk_ready, 1)

            def counts(L):
                pe.wait_ge(lg_read, (J + 1) * GROUPS * (L + 1))
                pe.wait_ge(pos_done, GROUPS * (L + 1))
                for t in range(TILES):
                    ins = pe.matmul(CN, ones[:, :], hot[:, t, :], start=(t == 0), stop=(t == TILES - 1))
                ins.then_inc(cn_ready, 1)

            def mask_transposes(e, b, slot_):
                pe.wait_ge(w_ready, e - 1 + W_CREDIT)
                for c in range(KC):
                    for k in range(KC):
                        at = k * D + c * P
                        ins = pe.transpose(PJ[b][:, at:at + P],
                                           mask_raw[:, slot_ // CHUNK, KC * (slot_ % CHUNK) + c, k * P:(k + 1) * P],
                                           ident[:, :])
                ins.then_inc(mask_T, 1)

            def rows_transposes(L, q, m):
                b = m % 2
                if isinstance(q, int) and q < 2:
                    pe.wait_ge(xt_out, XT_EXP[L] + q - 1)
                    if lo_before(XT_EXP[L] + q - 1) > 0:
                        pe.wait_ge(xt_lo, lo_before(XT_EXP[L] + q - 1))
                else:
                    pe.wait_ge(xt_lo, LO_EXP[L] + q - 1)
                for s in range(2):
                    for k in range(KC):
                        at = (s * KC + k) * P
                        ins = pe.transpose(XT[b][:, at:at + P], xs[:, 2 * m + s, k * P:(k + 1) * P], ident[:, :])
                ins.then_inc(xt_full, 1)

            def product(L, q, m):
                b = m % 2
                pe.wait_ge(xt_lo, LO_EXP[L] + q + 1)
                pe.wait_ge(y_out, PAIRS * L + q - 1 + Y_CREDIT)
                for s in range(2):
                    for k in range(KC):
                        for n, part in enumerate((xs_hi, xs_lo)):
                            ins = pe.matmul(O[b][:, s * D:(s + 1) * D], part[:, b, (s * KC + k) * P:(s * KC + k + 1) * P],
                                            w_exp[:, bass.ds(2 * q + s, 1), k, :].rearrange("p a o -> p (a o)"),
                                            start=(k == 0 and n == 0), stop=(k == KC - 1 and n == 1))
                ins.then_inc(y_full, 1)

            def expert_turn(L, i, masks, last=False):
                for m in range(BP):
                    q = BP * i + m
                    if m == 1:
                        pe.wait_ge(xs_in[1], 16 * (CHUNKS // 2 * L + i + 1))
                    if m == BP - 1 and not last:
                        pe.wait_ge(xs_in[0], 16 * (CHUNKS // 2 * L + i + 2))
                    if not (last and m == BP - 1):
                        rows_transposes(L, q + 1, (m + 1) % BP)
                    if masks:
                        if m % 2 == 0:
                            pe.wait_ge(mask_in[m // 2], 16 * (i + 1 + AHEAD // BODY))
                        for k in range(2):
                            mask_transposes(AHEAD + 2 * q + k, k, 2 * m + k)
                    product(L, q, m)

            def experts(L):
                pe.wait_ge(xs_in[0], 16 * (CHUNKS // 2 * L + 1))
                rows_transposes(L, 0, 0)
                if L == 0:
                    pe.wait_ge(w_ready, AHEAD + W_CREDIT)
                    with pe.Fori(0, AHEAD // BODY) as i:
                        expert_turn(L, i, True)
                    pe.wait_ge(w_ready, E + W_CREDIT)
                with pe.Fori((1 - L) * AHEAD // BODY, E // BODY - 1) as i:
                    expert_turn(L, i, False)
                expert_turn(L, E // BODY - 1, False, last=True)

            def rounds(L):
                with pe.If(rounds_needed(pe, L)):
                    v = rd[L]
                    pe.wait_ge(y_out, PAIRS * (L + 1) + Y_CREDIT)
                    with pe.Fori(0, ROUNDS * E) as n:
                        pe.wait_ge(v["rows"], 16 * (n + 1))
                        for k in range(KC):
                            pe.transpose(XT[0][:, k * P:(k + 1) * P], xs[:, 0, k * P:(k + 1) * P], ident[:, :])
                        pe.wait_ge(v["mask"], 16 * (n + 1))
                        for c in range(KC):
                            for k in range(KC):
                                at = k * D + c * P
                                ins = pe.transpose(PJ[0][:, at:at + P], mask_raw[:, 0, c, k * P:(k + 1) * P], ident[:, :])
                        ins.then_inc(v["T"], 1)
                        pe.wait_ge(v["xT"], n + 1)
                        pe.wait_ge(v["w"], n + 1)
                        for k in range(KC):
                            ins = pe.matmul(O[0][:, 0:D], xs_one[:, k, :], w_one[:, k, :],
                                            start=(k == 0), stop=(k == KC - 1))
                        ins.then_inc(v["y"], 1)
                    pe.wait_ge(v["yout"], ROUNDS * E)

            def project(g, c):
                pe.wait_ge(xt_lo, lo_before(XT_ATT[g] + 2))
                n = KC * g + c
                m = slice(c * P, (c + 1) * P)
                for w, ready, free in ((0, pg_ready, tg_done), (1, pv_ready, st_done), (2, pq_ready, tq_done)):
                    if n > 0:
                        pe.wait_ge(free, n)
                    for k in range(KC):
                        for a, (wx, xx) in enumerate(((w_hi, xa_hi), (w_hi, xa_lo), (w_lo, xa_hi))):
                            ins = pe.matmul(PJ[w][:, 0:GT], wx[:, w, k, m], xx[:, g % 2, k, :],
                                            start=(k == 0 and a == 0), stop=(k == KC - 1 and a == 2))
                    ins.then_inc(ready, 1)

            def out_project(g):
                pe.wait_ge(ld_lo_done, KC * (g + 1))
                for h in range(2):
                    if g > 0:
                        pe.wait_ge(x2_done, 2 * g)
                    for j in range(2):
                        t = slice((2 * h + j) * P, (2 * h + j + 1) * P)
                        for c in range(KC):
                            for a, (lx, wx) in enumerate(((load_hi, w_hi), (load_hi, w_lo), (load_lo, w_hi))):
                                ins = pe.matmul(O[h][:, j * D:(j + 1) * D], lx[:, c, t], wx[:, 3, c, :],
                                                start=(c == 0 and a == 0), stop=(c == KC - 1 and a == 2))
                    ins.then_inc(o_ready, 1)

            pe.sem_inc(y_full, Y_CREDIT)
            pe.wait_ge(ident_done, 1)
            pe.wait_ge(r_in, 16)
            for k in range(KC):
                ins = pe.transpose(PJ[0][:, k * E:(k + 1) * E], r_nat[:, k * P:(k + 1) * P], ident[0:E, 0:E])
            ins.then_inc(small_T, 1)

            transpose_ffn(0, 0)
            pe.wait_ge(small_ready, 1)
            logits(0, 0)
            transpose_ffn(0, 1)
            pe.wait_ge(below_done, 1)
            pe.wait_ge(consts_done, 3)
            for g in range(1, GROUPS):
                ranks(0, g - 1)
                logits(0, g)
                if g + 1 < GROUPS:
                    transpose_ffn(0, g + 1)
            pe.wait_ge(quant_done, 1)
            for c in range(KC):
                for k in range(KC):
                    ins = pe.transpose(PJ[0][:, k * D + c * P:k * D + (c + 1) * P], w_low[:, c, k * P:(k + 1) * P],
                                       ident[:, :])
            ins.then_inc(qT_full, 1)
            pe.wait_ge(b_in, 32)
            pe.transpose(PJ[1][:, 0:4], vec_rows[:, :], ident[0:4, 0:4]).then_inc(small_T, 1)
            ranks(0, GROUPS - 1)
            counts(0)
            pe.wait_ge(small_ready, 2)
            pe.wait_ge(qT_ready, 1)
            with pe.Fori(0, AHEAD // BODY) as i:
                for s in range(2):
                    pe.wait_ge(mask_in[s], 16 * (i + 1))
                    for m in range(CHUNK):
                        mask_transposes(BODY * i + CHUNK * s + m, m % 2, CHUNK * s + m)
            experts(0)
            pe.wait_ge(lowmax_done, 1)
            pe.wait_ge(most_done, 1)
            pe.matmul(LOW, ones_f[:, :], low_max[:, :], start=True, stop=True).then_inc(low_ready, 1)
            rounds(0)

            pe.wait_ge(w_lo_done, 1)
            pe.wait_ge(y_out, PAIRS + Y_CREDIT)
            transpose_mem(0)
            for i in range(GROUPS + 3):
                if i < GROUPS:
                    project(i, 0)
                if i + 1 < GROUPS:
                    transpose_mem(i + 1)
                if 0 <= i - 3 < GROUPS:
                    ranks(1, i - 3)
                if i < GROUPS:
                    project(i, 1)
                if 0 <= i - 1 < GROUPS:
                    out_project(i - 1)
                if 0 <= i - 2 < GROUPS:
                    transpose_ffn(1, i - 2)
                    logits(1, i - 2)
            counts(1)
            pe.wait_ge(x2_done, 2 * GROUPS)
            experts(1)
            rounds(1)


_INS = ["L0_attn_x", "L0_attn_Wv", "L0_attn_Wg", "L0_attn_bg", "L0_attn_Wq", "L0_attn_bq", "L0_attn_Wo",
        "L0_ffn_weight", "L0_ffn_scale", "L0_ffn_expert_masks", "L0_ffn_router_w"]


def kernel(**inputs):
    import concourse.bacc as bacc
    from concourse.bass_utils import run_bass_kernel_spmd

    nc = bacc.Bacc("TRN2", target_bir_lowering=False, num_devices=1)
    arrays, args = {}, []
    for name in _INS:
        a = np.ascontiguousarray(inputs[name])
        arrays[f"in_{name}"] = a
        args.append(nc.dram_tensor(f"in_{name}", a.shape, mybir.dt.from_np(a.dtype), kind="ExternalInput").ap())
    x = arrays["in_L0_attn_x"]
    out = nc.dram_tensor("out_x", x.shape, F32, kind="ExternalOutput").ap()
    macaron_block(nc, *args, out)
    r = run_bass_kernel_spmd(nc, [arrays], core_ids=[0])
    return r.results[0]["out_x"]
```

```python
from contextlib import ExitStack

import numpy as np
import concourse.bass as bass
from concourse import mybir

F32 = mybir.dt.float32
F32R = mybir.dt.float32r
BF16 = mybir.dt.bfloat16
I32 = mybir.dt.int32
U32 = mybir.dt.uint32
U16 = mybir.dt.uint16
ALU = mybir.AluOpType
ACT = mybir.ActivationFunctionType
AX = mybir.AxisListType

P = 128
EPS = 1e-5
DECAY = 0.95
THRESH = 0.5
TILES_PER_GROUP = 4
CHUNK = 4
BODY = 2 * CHUNK
AHEAD = 16


def macaron_block(nc, x, wv, wg, bg, wq, bq, wo, weight, scale, masks, router, out):
    B, S, D = x.shape
    E = masks.shape[0]
    TOKENS = B * S
    TILES = TOKENS // P
    J = TILES_PER_GROUP
    GROUPS = TILES // J
    GT = J * P
    SEQS = GT // S
    KC = D // P
    ROUNDS = TOKENS // P
    SKIP = 1 << 16
    CHUNKS = E // CHUNK
    PAIRS = E // 2
    BP = BODY // 2
    GATE = float(np.float32(np.sqrt(1.0 - DECAY))) ** 2 / 4
    assert D == KC * P and TILES == GROUPS * J and GT == SEQS * S and GT <= 512 and KC == 2
    assert E % BODY == 0 and J * E <= 128 and GROUPS == 4 and 2 * D <= 512 and AHEAD * 2 == E

    x_rows = x.rearrange("b s d -> (b s) d").rearrange("(t p) d -> p t d", p=P)
    mask_rows = masks.rearrange("e o i -> (e o) i").rearrange("(n p) i -> p n i", p=P)

    W = D + 2
    ROW = (W, W + D)
    xs_dram = [nc.dram_tensor(f"rows_by_expert{L}", (E * P, ROW[L]), F32, kind="Internal").ap() for L in range(2)]
    ys_dram = nc.dram_tensor("results_by_token", (TOKENS, D), F32, kind="Internal").ap()
    xs_tiles = [dram.rearrange("(e p) d -> p e d", p=P) for dram in xs_dram]
    ys_tiles = ys_dram.rearrange("(t p) d -> p t d", p=P)
    result_rows = (ys_dram, out.rearrange("b s d -> (b s) d"))
    LAST_ROW = E * P - 1
    assert 2 * TILES == E

    with ExitStack() as ctx:
        def sb(name, shape, dt=F32):
            return ctx.enter_context(nc.sbuf_tensor(name, shape, dt))

        def psum(name):
            return ctx.enter_context(nc.psum_tensor(name, [P, 512], F32))

        def sem(name):
            return ctx.enter_context(nc.semaphore(name))

        def sems(*names):
            return [sem(name) for name in names]

        w_exp = sb("w_exp", [P, E, KC, D], F32R)
        xs = sb("xs", [P, BODY, W])
        ys = sb("ys", [P, BODY, D])
        tok = sb("tok", [P, TILES, ROW[1]])
        xf = tok[:, :, 0:W]
        xt = tok[:, :, W:W + D]
        x_exp = tok[:, :, :].rearrange("p t d -> p (t d)")[:, 0:E * D].rearrange("p (e d) -> p e d", d=D)
        hw = sb("hw", [P, E])
        ids = sb("ids", [P, E], U32)
        xfT = sb("xfT", [P, KC, GT])
        xa_hi = sb("xa_hi", [P, 2, KC, GT], F32R)
        xa_lo = sb("xa_lo", [P, 2, KC, GT], F32R)
        mask_raw = sb("mask_raw", [P, 2, KC * CHUNK, D])
        xa = mask_raw[:, 0, 0:J, :]
        low_sum = sb("low_sum", [P, E])
        low_max = sb("low_max", [P, 1])
        w_hi = sb("w_hi", [P, 4, KC, D], F32R)
        w_lo = sb("w_lo", [P, 4, KC, D], F32R)
        work = sb("work", [P, 4, KC, GT])
        tanh_g, tanh_q, store, mem = (work[:, i] for i in range(4))
        w_raw = work[:, 0:2].rearrange("p a k t -> p (a k t)").rearrange("p (w k d) -> p w k d", w=4, k=KC)
        load = sb("load", [P, KC, GT])
        low_bits = load[:, 0, 0:KC * D].bitcast(BF16).rearrange("p (b n) -> p b n", b=2)
        load_hi = sb("load_hi", [P, KC, GT], F32R)
        load_lo = sb("load_lo", [P, KC, GT], F32R)
        xs_hi, xs_lo = load_hi, load_lo
        x_one = work[:, 0, 0, 0:D]
        xs_one = load[:, 0, 0:KC * P].rearrange("p (k c) -> p k c", k=KC)
        w_one = load[:, 1, 0:KC * D].rearrange("p (k o) -> p k o", k=KC)
        early_masks = [mask_raw[:, 0], mask_raw[:, 1],
                       work[:, 2:4].rearrange("p a k t -> p (a k t)").rearrange("p (n d) -> p n d", d=D), ys[:, :, :]]
        w_nat = xs[:, 0:KC, 0:D]
        w_low = xs[:, KC:2 * KC, 0:D]
        w_qT = sb("w_qT", [P, KC, D])
        scale_b = sb("scale_b", [P, D])
        r_nat = sb("r_nat", [E, D])
        rT = sb("rT", [P, KC, E])
        vec_rows = sb("vec_rows", [4, P])
        half_b = sb("half_b", [P, 4])
        ident = sb("ident", [P, P])
        ones_f = sb("ones_f", [P, W])
        below = sb("below", [P, P], BF16)
        ones = sb("ones", [P, P], BF16)
        iota_e = sb("iota_e", [P, E], I32)
        expert = sb("expert", [P, E], BF16)
        prefer = sb("prefer", [P, E])
        decay = sb("decay", [P, S])
        neg_half = sb("neg_half", [P, J])
        NI = 3 * GROUPS
        stats = sb("stats", [P, NI, J, 6])
        mv = sb("mv", [P, NI, J, 2])
        var_eps = sb("var_eps", [P, NI, J])
        rstd = sb("rstd", [P, NI, J])
        nmr = sb("nmr", [P, NI, J])
        top = sb("top", [P, TILES])
        lm = sb("lm", [P, TILES, E])
        cand = sb("cand", [P, J, E])
        best = sb("best", [P, J])
        hot = sb("hot", [P, TILES, E], BF16)
        pos = sb("pos", [P, J, E])
        slot = sb("slot", [P, TILES])
        limit = sb("limit", [P, TILES])
        late = sb("late", [P, TILES])
        early = sb("early", [P, TILES])
        row = sb("row", [P, TILES], U32)
        esum = sb("esum", [P, TILES])
        prob = sb("prob", [P, TILES])
        half_w = sb("half_w", [P, TILES])
        most = sb("most", [P, 2])
        over_f = sb("over_f", [P, 2])
        low_f = sb("low_f", [P, 1])
        flag = sb("flag", [P, 2], I32)

        XT = [psum("XT0"), psum("XT1")]
        PJ = [psum("PG"), psum("PV"), psum("PQ")]
        O = [psum("O0"), psum("O1")]
        RT = psum("RT")
        LG = [[O[g % 2][:, 0:J * E] for g in range(GROUPS)],
              [(RT if g < 2 else PJ[0])[:, 0:J * E] for g in range(GROUPS)]]
        RK = [[PJ[2][:, 0:J * E]] * GROUPS,
              [RT[:, J * E:2 * J * E] if g < 1 else PJ[2][:, 0:J * E] for g in range(GROUPS)]]
        CN = RT[:, 2 * J * E:2 * J * E + E]
        LOW = RT[:, 2 * J * E + E:2 * J * E + E + 1]

        x_in = sems(*[f"x_in{g}" for g in range(GROUPS)])
        w_in, r_in, b_in, scale_in, att_in = sems("w_in", "r_in", "b_in", "scale_in", "att_in")
        mask_in = sems("mask_in0", "mask_in1", "mask_in2", "mask_in3")
        ids_set, cleared = sems("ids_set", "cleared")
        iota_done, ident_done, ones_f_done, below_done = sems("iota_done", "ident_done", "ones_f_done", "below_done")
        ones_done, consts_done, neg_half_done = sems("ones_done", "consts_done", "neg_half_done")
        small_T, small_ready, low_done, quant_done = sems("small_T", "small_ready", "low_done", "quant_done")
        qT_full, qT_ready, wo_scaled, w_hi_done, w_lo_done = sems("qT_full", "qT_ready", "wo_scaled", "w_hi_done",
                                                                  "w_lo_done")
        mask_T, mask_tested, w_ready = sems("mask_T", "mask_tested", "w_ready")
        ln = {k: {s: sem(f"ln{k}_{s}") for s in ("stats", "mv", "var", "rstd", "nmr", "xn")} for k in "FA"}
        xt_full, xt_out, xt_lo = sems("xt_full", "xt_out", "xt_lo")
        lg_ready, top_done, lg_read, cand_done = sems("lg_ready", "top_done", "lg_read", "cand_done")
        best_done, hot_done, rk_ready, pos_done = sems("best_done", "hot_done", "rk_ready", "pos_done")
        slot_done, limit_done, late_done, row_done = sems("slot_done", "limit_done", "late_done", "row_done")
        scattered, cn_ready, most_done, over_done = sems("scattered", "cn_ready", "most_done", "over_done")
        lowmax_done, low_ready, low_f_done, flag_done = sems("lowmax_done", "low_ready", "low_f_done", "flag_done")
        exp_done, esum_done, prob_done, half_done = sems("exp_done", "esum_done", "prob_done", "half_done")
        xs_in = sems("xs_in0", "xs_in1")
        y_full, y_out, y_read, y_final, x_exp_in = sems("y_full", "y_out", "y_read", "y_final", "x_exp_in")
        ids_taken, turns, sp_turns = sems("ids_taken", "turns", "sp_turns")
        returned = sems("returned0", "returned1")
        loaded = sems(*[f"loaded{g}" for g in range(GROUPS)])
        x1_done, x2_done = sems("x1_done", "x2_done")
        pg_ready, pv_ready, pq_ready = sems("pg_ready", "pv_ready", "pq_ready")
        tg_done, tq_done, st_done, mem_done = sems("tg_done", "tq_done", "st_done", "mem_done")
        ld_done, ld_hi_done, ld_lo_done, o_ready = sems("ld_done", "ld_hi_done", "ld_lo_done", "o_ready")
        rd = [{s: sem(f"rounds{L}_{s}") for s in ("ids", "cur", "edge", "row", "scat", "row_free", "tile_free", "rows", "mask",
                                                  "T", "xT", "w", "y", "yread", "yout", "back", "cleared")} for L in range(2)]

        F, A = [("F", False)] * 2, [("A", True)] * 2
        uses = GROUPS * F + [("E", True)] * PAIRS + A
        XT_EXP = [GROUPS * 2, 0]
        XT_ATT, XT_FFN = [XT_EXP[0] + PAIRS], [[2 * g for g in range(GROUPS)], []]
        for i in range(GROUPS + 2):
            if i + 1 < GROUPS:
                XT_ATT.append(len(uses))
                uses = uses + A
            if i >= 2:
                XT_FFN[1].append(len(uses))
                uses = uses + F
        XT_EXP[1] = len(uses)
        uses = uses + [("E", True)] * PAIRS

        def lo_before(u):
            return sum(lo for _, lo in uses[:u])

        LO_EXP = [lo_before(XT_EXP[L]) for L in range(2)]
        Y_CREDIT, W_CREDIT, M_CREDIT = 2, 2, 2

        def tiles(g):
            return slice(g * J, (g + 1) * J)

        def taken(L, n):
            return CHUNKS * L + (1 + L) * n

        def new_masks(L, i, m, last):
            if L == 1 or last and m >= 2:
                return []
            places = [(m, 0), (m, 1)] if last else [(m // 2, m % 2)]
            return [(AHEAD + CHUNK * i + 2 * b + k, b, k) for b, k in places]

        def rounds_needed(eng, L):
            eng.wait_ge(flag_done, L + 1)
            return eng.value_load(flag[0:1, L:L + 1], min_val=0, max_val=1) > 0

        block = ctx.enter_context(nc.Block())

        @block.sync
        def _(sp):
            def load_masks(c, b, dst):
                sp.dma_start(dst, mask_rows[:, c * KC * CHUNK:(c + 1) * KC * CHUNK, :]).then_inc(mask_in[b], 16)

            def clear_rows(L, done):
                for c in range(E // BODY):
                    for at, width in ((0, W), (W, D))[0:L + 1]:
                        sp.dma_start(xs_tiles[L][:, c * BODY:(c + 1) * BODY, at:at + width],
                                     ones_f[:, 0:width].unsqueeze(1).to_broadcast([P, BODY, width])).then_inc(done, 16)

            for g in range(GROUPS):
                sp.dma_start(xt[:, tiles(g), :], x_rows[:, tiles(g), :]).then_inc(x_in[g], 16)
                if g == 0:
                    sp.dma_start(r_nat[:, :], router).then_inc(r_in, 16)
                if g == 1:
                    sp.dma_start(w_nat, weight.rearrange("(c p) i -> p c i", p=P)).then_inc(w_in, 16)
                    for k, v in enumerate((bg, bq)):
                        sp.dma_start(vec_rows[2 * k:2 * k + 2, :], v.rearrange("(c p) -> c p", p=P)).then_inc(b_in, 16)
            sp.wait_ge(ones_f_done, 1)
            clear_rows(0, cleared)
            for c in range(AHEAD // CHUNK):
                load_masks(c, c, early_masks[c])
            sp.dma_start(scale_b[:, :], scale.partition_broadcast(P)).then_inc(scale_in, 16)
            for k, w in enumerate((wg, wv, wq, wo)):
                sp.dma_start(w_raw[:, k], w.rearrange("(c p) m -> p c m", p=P)).then_inc(att_in, 16)

            def next_masks(i, b):
                last = CHUNK * (b + 1) if isinstance(i, int) and i == 0 else AHEAD + CHUNK * (i - 1) + 2 * (b + 1)
                sp.wait_ge(mask_T, last)
                sp.sem_inc(sp_turns, 1)
                sp.wait_ge(mask_tested, M_CREDIT + last)
                sp.dma_start(mask_raw[:, b, 0:2 * KC], mask_rows[:, bass.ds((AHEAD + CHUNK * i + 2 * b) * KC, 2 * KC), :]
                             ).then_inc(mask_in[b], 16)

            def load_rows(L, c, b):
                sp.dma_start(xs[:, b * CHUNK:(b + 1) * CHUNK, :],
                             xs_tiles[L][:, bass.ds(c * CHUNK, CHUNK), 0:W]).then_inc(xs_in[b], 16)

            def next_rows(L, c, b):
                sp.wait_ge(xt_full, XT_EXP[L] + CHUNK // 2 * (c - 1))
                sp.sem_inc(sp_turns, 1)
                sp.wait_ge(ids_taken, taken(L, c - 1))
                load_rows(L, c, b)

            def rounds(L):
                with sp.If(rounds_needed(sp, L)):
                    v = rd[L]
                    with sp.Fori(0, ROUNDS) as r:
                        with sp.Fori(0, E) as e:
                            n = r * E + e
                            sp.wait_ge(v["scat"], 16 * TILES * (r + 1))
                            sp.sem_inc(sp_turns, 1)
                            sp.wait_ge(v["tile_free"], n + 1)
                            sp.dma_start(xs[:, 0:1, :], xs_tiles[L][:, bass.ds(e, 1), 0:W]).then_inc(v["rows"], 16)
                            if L == 1:
                                sp.dma_start(x_one.unsqueeze(1), xs_tiles[L][:, bass.ds(e, 1), W:W + D]
                                             ).then_inc(v["rows"], 16)
                            sp.dma_start(mask_raw[:, 0, 0:KC, :], mask_rows[:, bass.ds(e * KC, KC), :]
                                         ).then_inc(v["mask"], 16)
                    sp.wait_ge(v["tile_free"], ROUNDS * E + 1)
                    if L == 1:
                        clear_rows(L, v["cleared"])
                        sp.wait_ge(v["cleared"], 2 * 16 * (E // BODY))

            next_masks(0, 0)
            sp.wait_ge(cleared, 16 * (E // BODY))
            sp.wait_ge(qT_full, 1)
            sp.wait_ge(scattered, 16 * TILES)
            load_rows(0, 0, 0)
            load_rows(0, 1, 1)
            next_masks(0, 1)
            with sp.Fori(0, E // BODY - 1) as i:
                for b in range(2):
                    next_rows(0, 2 * i + b + 2, b)
                    next_masks(i + 1, b)
            for b in range(2):
                sp.wait_ge(returned[b], 16 * E // 2)
            rounds(0)
            for g in range(GROUPS):
                sp.dma_start(xf[:, tiles(g), 0:D], ys_tiles[:, tiles(g), :]).then_inc(loaded[g], 16)
            clear_rows(1, cleared)

            rounds(1)
            sp.wait_ge(scattered, 2 * 16 * TILES)
            load_rows(1, 0, 0)
            load_rows(1, 1, 1)
            for i in range(E // BODY):
                if i > 0:
                    next_rows(1, 2 * i, 0)
                    sp.wait_ge(x_exp_in, 16 * i)
                sp.dma_start(x_exp[:, i * BODY:(i + 1) * BODY, :],
                             xs_tiles[1][:, i * BODY:(i + 1) * BODY, W:W + D]).then_inc(x_exp_in, 16)
                if i > 0:
                    next_rows(1, 2 * i + 1, 1)
            for b in range(2):
                sp.wait_ge(returned[b], 16 * E)

        @block.gpsimd
        def _(pool):
            pool.memset(ones_f[:, :], 1.0).then_inc(ones_f_done, 1)
            pool.memset(neg_half[:, :], -0.5).then_inc(neg_half_done, 1)
            pool.wait_ge(ones_f_done, 1)
            pool.affine_select(out=ident[:, :], in_=ones_f[:, 0:P], pattern=[[1, P]], compare_op=ALU.is_equal,
                               fill=0.0, base=0, channel_multiplier=-1).then_inc(ident_done, 1)
            pool.iota(iota_e[:, :], pattern=[[1, E]], base=0, channel_multiplier=0).then_inc(iota_done, 1)
            pool.wait_ge(ones_done, 1)
            pool.affine_select(out=below[:, :], in_=ones[:, :], pattern=[[1, P]], compare_op=ALU.is_gt,
                               fill=0.0, base=0, channel_multiplier=-1).then_inc(below_done, 1)
            pool.wait_ge(neg_half_done, 1)

            def inv_std(kind, n, q):
                pool.wait_ge(ln[kind]["var"], n + 1)
                pool.tensor_tensor(rstd[:, q, :], var_eps[:, q, :], neg_half[:, :], ALU.pow).then_inc(ln[kind]["rstd"], 1)

            def scatter_tile(L, t, done):
                pool.indirect_dma_start(xs_dram[L], bass.IndirectOffsetOnAxis(ap=row[:, t:t + 1], axis=0), tok[:, t, 0:ROW[L]],
                                        None, bounds_check=LAST_ROW, oob_is_err=False).then_inc(done, 16)

            def return_rows(L, b, src, done):
                pool.indirect_dma_start(result_rows[L], bass.IndirectOffsetOnAxis(ap=ids[:, b:b + 1], axis=0), src,
                                        None, bounds_check=TOKENS - 1, oob_is_err=False).then_inc(done, 16)

            def set_ids():
                pool.iota(xf[:, :, D].bitcast(I32), pattern=[[P, TILES]], base=0, channel_multiplier=1).then_inc(ids_set, 1)
                pool.memset(xf[:, :, D + 1:D + 2], 0.0).then_inc(ids_set, 1)

            def scatter(L, g):
                n = L * GROUPS + g
                pool.wait_ge(ids_set, 2)
                if L == 1:
                    pool.wait_ge(cleared, 3 * 16 * (E // BODY))
                    pool.wait_ge(half_done, g + 2)
                    pool.wait_ge(x2_done, 2 * (g + 1))
                pool.wait_ge(row_done, n + 1)
                pool.wait_ge(ln["F"]["xn"], J * (n + 1))
                for t in range(g * J, (g + 1) * J):
                    scatter_tile(L, t, scattered)

            def take_ids(L, c):
                pool.wait_ge(xs_in[c % 2], 16 * (CHUNKS // 2 * L + c // 2 + 1))
                in_xs, of_all = slice(c % 2 * CHUNK, (c % 2 + 1) * CHUNK), slice(c * CHUNK, (c + 1) * CHUNK)
                pool.tensor_copy(ids[:, of_all], xs[:, in_xs, D].bitcast(U32)).then_inc(ids_taken, 1)
                if L == 1:
                    pool.tensor_copy(hw[:, of_all], xs[:, in_xs, D + 1]).then_inc(ids_taken, 1)

            def return_results(L):
                if L == 1:
                    for b in range(2):
                        pool.wait_ge(returned[b], 16 * E // 2)
                for c in range(2):
                    take_ids(L, c)
                for c in range(CHUNKS):
                    pool.wait_ge(ids_taken, taken(L, c + 1))
                    for s in range(CHUNK):
                        e = c * CHUNK + s
                        if L == 0:
                            pool.wait_ge(y_out, Y_CREDIT + e // 2 + 1)
                            return_rows(L, e, ys[:, e % BODY, :], returned[c % 2])
                        else:
                            pool.wait_ge(y_final, e + 1)
                            return_rows(L, e, x_exp[:, e, :], returned[c % 2])
                        if s == CHUNK - 2 and c + 2 < CHUNKS:
                            take_ids(L, c + 2)

            def rounds(L):
                with pool.If(rounds_needed(pool, L)):
                    v = rd[L]
                    for b in range(2):
                        pool.wait_ge(returned[b], 16 * E // 2)
                    pool.wait_ge(scattered, 16 * TILES * (L + 1))
                    pool.sem_inc(v["row_free"], 1)
                    pool.sem_inc(v["tile_free"], 1)
                    with pool.Fori(0, ROUNDS) as r:
                        pool.wait_ge(v["row"], r + 1)
                        pool.sem_inc(turns, 1)
                        for t in range(TILES):
                            scatter_tile(L, t, v["scat"])
                        pool.wait_ge(v["scat"], 16 * TILES * (r + 1))
                        pool.sem_inc(v["row_free"], 1)
                        with pool.Fori(0, E) as e:
                            n = r * E + e
                            pool.wait_ge(v["yout"], n + 1)
                            pool.sem_inc(turns, 1)
                            pool.tensor_copy(ids[:, 0:1], xs[:, 0, D:D + 1].bitcast(U32)).then_inc(v["ids"], 1)
                            pool.wait_ge(v["ids"], n + 1)
                            pool.sem_inc(turns, 1)
                            return_rows(L, 0, ys[:, 0, :], v["back"])
                            pool.wait_ge(v["back"], 16 * (n + 1))
                            pool.sem_inc(v["tile_free"], 1)

            def split_load(g):
                for c in range(KC):
                    pool.wait_ge(ld_hi_done, KC * g + c + 1)
                    if g > 0:
                        pool.wait_ge(o_ready, 2 * g)
                    pool.tensor_tensor(load_lo[:, c, :], load[:, c, :], load_hi[:, c, :], ALU.subtract
                                       ).then_inc(ld_lo_done, 1)

            set_ids()
            for g in range(GROUPS):
                inv_std("F", g, g)
            pool.wait_ge(cleared, 16 * (E // BODY))
            for g in range(GROUPS):
                scatter(0, g)
            return_results(0)
            rounds(0)
            QA = 2 * GROUPS
            inv_std("A", 0, QA)
            inv_std("A", 1, QA + 1)
            for i in range(GROUPS + 3):
                if 0 <= i - 1 < GROUPS:
                    split_load(i - 1)
                if i + 2 < GROUPS:
                    inv_std("A", i + 2, QA + i + 2)
                if i == 3:
                    scatter(1, 0)
                if 0 <= i - 1 < GROUPS:
                    inv_std("F", GROUPS + i - 1, GROUPS + i - 1)
                if i > 3:
                    scatter(1, i - 3)
            rounds(1)
            return_results(1)

        @block.scalar
        def _(act):
            def normalise(kind, n, q, g, dst):
                act.wait_ge(ln[kind]["nmr"], n + 1)
                for j in range(J):
                    act.activation(dst[:, j, :], xt[:, g * J + j, :], ACT.Identity, bias=nmr[:, q, j:j + 1],
                                   scale=rstd[:, q, j:j + 1]).then_inc(ln[kind]["xn"], 1)

            def normalise_ffn(L, g):
                n = L * GROUPS + g
                if L == 1:
                    act.wait_ge(x1_done, J * (g + 1))
                normalise("F", n, n, g, xf[:, tiles(g), 0:D])

            def normalise_mem(g):
                if g > 0:
                    act.wait_ge(xt_full, XT_ATT[g - 1] + 2)
                normalise("A", g, 2 * GROUPS + g, g, xa)

            def copy_T(u, dst):
                for h in range(2):
                    act.wait_ge(xt_full, u + h + 1)
                    act.copy(dst[:, :, h * 2 * P:(h + 1) * 2 * P].rearrange("p k (j c) -> p k j c", j=2),
                             XT[h][:, :].rearrange("p (j k c) -> p k j c", j=2, k=KC)).then_inc(xt_out, 1)

            def copy_T_ffn(L, g):
                n = L * GROUPS + g
                if n > 0:
                    act.wait_ge(lg_ready, n)
                copy_T(XT_FFN[L][g], xfT)

            def copy_T_mem(g):
                if g > 1:
                    act.wait_ge(pq_ready, KC * (g - 1))
                copy_T(XT_ATT[g], xa_hi[:, g % 2])

            def exponentials(L, groups):
                act.wait_ge(lg_read, (J + 1) * (GROUPS * L + groups.stop // J))
                act.activation(lm[:, groups, :], lm[:, groups, :], ACT.Exp).then_inc(exp_done, 1)

            def test_mask(e, b, masks, m):
                act.wait_ge(mask_tested, e - 1 + M_CREDIT)
                act.activation(low_bits[:, b], masks[:, KC * m:KC * (m + 1), :].rearrange("p c i -> p (c i)")
                               .bitcast(U16).rearrange("p (n h) -> p n h", h=2)[:, :, 0],
                               ACT.Copy, accum_out=low_sum[:, bass.ds(e, 1)]).then_inc(mask_tested, 1)

            def test_chunk(c):
                act.wait_ge(mask_in[c], 16)
                for m in range(CHUNK):
                    test_mask(CHUNK * c + m, m % 2, early_masks[c], m)

            def round_rows(L, q, b):
                act.wait_ge(xt_full, XT_EXP[L] + q + 1)
                act.wait_ge(y_full, PAIRS * L + q - 1 + Y_CREDIT)
                act.copy(xs_hi[:, b, :], XT[b][:, :]).then_inc(xt_out, 1)

            def expert_turn(L, i, last=False):
                for m in range(BP):
                    if not (last and m == BP - 1):
                        round_rows(L, BP * i + m + 1, (m + 1) % 2)
                    for e, b, k in new_masks(L, i, m, last):
                        if k == 0:
                            act.wait_ge(mask_in[b], 16 * (i + 2))
                        test_mask(e, k, mask_raw[:, b], k)

            def experts(L):
                round_rows(L, 0, 0)
                with act.Fori(0, E // BODY - 1) as i:
                    expert_turn(L, i)
                expert_turn(L, E // BODY - 1, last=True)

            def rounds(L):
                with act.If(rounds_needed(act, L)):
                    v = rd[L]
                    with act.Fori(0, ROUNDS * E) as n:
                        act.wait_ge(v["T"], n + 1)
                        act.copy(xs_one[:, :, :], XT[0][:, 0:KC * P].rearrange("p (k c) -> p k c", k=KC)).then_inc(v["xT"], 1)

            def tanhs(g, c):
                n = KC * g + c
                act.wait_ge(pg_ready, n + 1)
                if g > 0:
                    act.wait_ge(st_done, KC * g)
                    act.wait_ge(ld_done, KC * g)
                act.activation(tanh_g[:, c, :], PJ[0][:, 0:GT], ACT.Tanh, bias=half_b[:, c:c + 1],
                               scale=0.5).then_inc(tg_done, 1)
                act.wait_ge(pq_ready, n + 1)
                act.activation(tanh_q[:, c, :], PJ[2][:, 0:GT], ACT.Tanh, bias=half_b[:, 2 + c:3 + c],
                               scale=0.5).then_inc(tq_done, 1)

            def round_load(g, c):
                n = KC * g + c
                act.wait_ge(ld_done, n + 1)
                if g > 0:
                    act.wait_ge(o_ready, 2 * g)
                act.copy(load_hi[:, c, :], load[:, c, :]).then_inc(ld_hi_done, 1)

            act.sem_inc(mask_tested, M_CREDIT)
            normalise_ffn(0, 0)
            normalise_ffn(0, 1)
            copy_T_ffn(0, 0)
            normalise_ffn(0, 2)
            copy_T_ffn(0, 1)
            normalise_ffn(0, 3)
            copy_T_ffn(0, 2)
            test_chunk(0)
            copy_T_ffn(0, 3)
            for c in range(1, AHEAD // CHUNK):
                test_chunk(c)
            exponentials(0, slice(0, TILES))
            experts(0)
            act.wait_ge(att_in, 64)
            act.wait_ge(wo_scaled, 1)
            act.copy(w_hi[:, :, :, :], w_raw).then_inc(w_hi_done, 1)
            rounds(0)

            normalise_mem(0)
            copy_T_mem(0)
            for i in range(GROUPS + 3):
                if 0 <= i - 1 < GROUPS:
                    for c in range(KC):
                        round_load(i - 1, c)
                if i > 3:
                    exponentials(1, tiles(i - 3))
                if i + 1 < GROUPS:
                    normalise_mem(i + 1)
                if i < GROUPS:
                    tanhs(i, 0)
                if i + 1 < GROUPS:
                    copy_T_mem(i + 1)
                if i == 3:
                    exponentials(1, tiles(0))
                if 0 <= i - 2 < GROUPS:
                    normalise_ffn(1, i - 2)
                if i < GROUPS:
                    tanhs(i, 1)
                if 0 <= i - 2 < GROUPS:
                    copy_T_ffn(1, i - 2)
            rounds(1)
            experts(1)

        @block.vector
        def _(dve):
            def norm_stats(kind, n, q, g):
                s = ln[kind]
                for j in range(J):
                    dve.bn_stats(stats[:, q, j, :], xt[:, g * J + j, :]).then_inc(s["stats"], 1)
                for j in range(J):
                    dve.wait_ge(s["stats"], J * n + j + 1)
                    dve.bn_aggr(mv[:, q, j, :], stats[:, q, j, :]).then_inc(s["mv"], 1)
                dve.wait_ge(s["mv"], J * (n + 1))
                dve.tensor_scalar(var_eps[:, q, :], mv[:, q, :, 1], EPS, None, ALU.add).then_inc(s["var"], 1)

            def norm_bias(kind, n, q):
                dve.wait_ge(ln[kind]["rstd"], n + 1)
                dve.scalar_tensor_tensor(out=nmr[:, q, :], in0=mv[:, q, :, 0], scalar=-1.0, in1=rstd[:, q, :],
                                         op0=ALU.mult, op1=ALU.mult).then_inc(ln[kind]["nmr"], 1)

            def choose(L, g):
                n = L * GROUPS + g
                lg = LG[L][g].rearrange("p (j e) -> p j e", j=J)
                dve.wait_ge(lg_ready, n + 1)
                dve.tensor_reduce(top[:, tiles(g)], lg, AX.X, ALU.max).then_inc(top_done, 1)
                dve.wait_ge(top_done, n + 1)
                for j in range(J):
                    dve.scalar_tensor_tensor(out=cand[:, j, :], in0=lg[:, j, :], scalar=top[:, g * J + j:g * J + j + 1],
                                             in1=prefer[:, :], op0=ALU.is_equal, op1=ALU.mult).then_inc(lg_read, 1)
                dve.tensor_tensor(lm[:, tiles(g), :], lg, top[:, tiles(g)].unsqueeze(2).to_broadcast([P, J, E]),
                                  ALU.subtract).then_inc(lg_read, 1)
                dve.wait_ge(lg_read, (J + 1) * n + J)
                dve.tensor_reduce(best[:, :], cand[:, :, :], AX.X, ALU.max).then_inc(best_done, 1)
                dve.wait_ge(best_done, n + 1)
                dve.tensor_tensor(hot[:, tiles(g), :], cand[:, :, :],
                                  best[:, :].unsqueeze(2).to_broadcast([P, J, E]), ALU.is_equal).then_inc(hot_done, 1)
                dve.tensor_scalar(limit[:, tiles(g)], best[:, :], -float(P), float((E + 1) * P), ALU.mult,
                                  ALU.add).then_inc(limit_done, 1)

            def number(L, g):
                n = L * GROUPS + g
                dve.wait_ge(rk_ready, n + 1)
                dve.tensor_tensor(pos[:, :, :], hot[:, tiles(g), :], RK[L][g].rearrange("p (j e) -> p j e", j=J),
                                  ALU.mult).then_inc(pos_done, 1)
                dve.wait_ge(pos_done, n + 1)
                dve.tensor_reduce(slot[:, tiles(g)], pos[:, :, :], AX.X, ALU.add).then_inc(slot_done, 1)
                dve.wait_ge(slot_done, n + 1)
                dve.wait_ge(limit_done, n + 1)
                dve.tensor_tensor(late[:, tiles(g)], slot[:, tiles(g)], limit[:, tiles(g)],
                                  ALU.is_ge).then_inc(late_done, 1)
                dve.wait_ge(late_done, n + 1)
                dve.scalar_tensor_tensor(out=row[:, tiles(g)], in0=late[:, tiles(g)], scalar=float(SKIP),
                                         in1=slot[:, tiles(g)], op0=ALU.mult, op1=ALU.add).then_inc(row_done, 1)

            def too_many(L):
                dve.wait_ge(cn_ready, L + 1)
                dve.tensor_reduce(most[:, L:L + 1], CN, AX.X, ALU.max).then_inc(most_done, 1)
                dve.wait_ge(most_done, L + 1)
                dve.tensor_scalar(over_f[:, L:L + 1], most[:, L:L + 1], float(P), None, ALU.is_gt).then_inc(over_done, 1)

            def masks_have_low_bits():
                dve.wait_ge(mask_tested, M_CREDIT + E)
                dve.tensor_reduce(low_max[:, :], low_sum[:, :], AX.X, ALU.max).then_inc(lowmax_done, 1)
                dve.wait_ge(low_ready, 1)
                dve.tensor_scalar(low_f[:, :], LOW, 0.0, None, ALU.is_gt).then_inc(low_f_done, 1)

            def set_flag(L):
                dve.wait_ge(over_done, L + 1)
                dve.wait_ge(low_f_done, 1)
                dve.tensor_tensor(flag[:, L:L + 1], over_f[:, L:L + 1], low_f[:, :], ALU.max).then_inc(flag_done, 1)

            def rounds(L):
                with dve.If(rounds_needed(dve, L)):
                    v = rd[L]
                    with dve.Fori(0, ROUNDS) as r:
                        dve.tensor_tensor(late[:, :], slot[:, :], limit[:, :], ALU.is_ge).then_inc(v["edge"], 1)
                        dve.scalar_tensor_tensor(out=early[:, :], in0=slot[:, :], scalar=float(P), in1=limit[:, :],
                                                 op0=ALU.add, op1=ALU.is_lt).then_inc(v["edge"], 1)
                        dve.wait_ge(v["edge"], 3 * r + 2)
                        dve.tensor_tensor(late[:, :], late[:, :], early[:, :], ALU.add).then_inc(v["edge"], 1)
                        dve.wait_ge(v["edge"], 3 * r + 3)
                        dve.wait_ge(v["row_free"], r + 1)
                        dve.scalar_tensor_tensor(out=row[:, :], in0=late[:, :], scalar=float(SKIP), in1=slot[:, :],
                                                 op0=ALU.mult, op1=ALU.add).then_inc(v["row"], 1)
                        dve.wait_ge(v["row"], r + 1)
                        dve.tensor_scalar(slot[:, :], slot[:, :], -float(P), None, ALU.add).then_inc(v["cur"], 1)
                        with dve.Fori(0, E) as e:
                            n = r * E + e
                            dve.wait_ge(v["T"], n + 1)
                            dve.tensor_tensor(w_one[:, :, :], PJ[0][:, :].rearrange("p (k o) -> p k o", k=KC),
                                              w_qT[:, :, :], ALU.mult).then_inc(v["w"], 1)
                            dve.wait_ge(v["y"], n + 1)
                            dve.wait_ge(v["tile_free"], n + 1)
                            dve.tensor_tensor(ys[:, 0, :], O[0][:, 0:D], scale_b[:, :], ALU.mult
                                              ).then_inc(v["yread" if L == 1 else "yout"], 1)
                            if L == 1:
                                dve.wait_ge(v["yread"], n + 1)
                                dve.scalar_tensor_tensor(out=ys[:, 0, :], in0=ys[:, 0, :], scalar=xs[:, 0, D + 1:D + 2],
                                                         in1=x_one, op0=ALU.mult, op1=ALU.add).then_inc(v["yout"], 1)
                        dve.wait_ge(v["cur"], r + 1)
                    dve.wait_ge(v["row_free"], ROUNDS + 1)

            def top_weights(k, groups, dst):
                dve.wait_ge(exp_done, k + 1)
                dve.tensor_reduce(esum[:, groups], lm[:, groups, :], AX.X, ALU.add).then_inc(esum_done, 1)
                dve.wait_ge(esum_done, k + 1)
                dve.reciprocal(prob[:, groups], esum[:, groups]).then_inc(prob_done, 1)
                dve.wait_ge(prob_done, k + 1)
                dve.tensor_scalar(dst, prob[:, groups], 0.5, None, ALU.mult).then_inc(half_done, 1)

            def top_weights_group(g):
                top_weights(g + 1, tiles(g), xf[:, tiles(g), D + 1])

            def build_weight(e, b):
                dve.wait_ge(mask_T, e + 1)
                dve.tensor_tensor(w_exp[:, bass.ds(e, 1), :, :].rearrange("p a k o -> p (a k) o"),
                                  PJ[b][:, :].rearrange("p (k o) -> p k o", k=KC), w_qT[:, :, :],
                                  ALU.mult).then_inc(w_ready, 1)

            def low_rows(L, q, b):
                dve.wait_ge(xt_out, XT_EXP[L] + q + 1)
                dve.tensor_tensor(xs_lo[:, b, :], XT[b][:, :],
                                  xs_hi[:, b, :], ALU.subtract).then_inc(xt_lo, 1)

            def scale_results(q, m):
                dve.wait_ge(y_full, Y_CREDIT + q + 1)
                dve.tensor_tensor(ys[:, 2 * m:2 * m + 2, :], O[m % 2][:, :].rearrange("p (e d) -> p e d", e=2),
                                  scale_b[:, :].unsqueeze(1).to_broadcast([P, 2, D]), ALU.mult).then_inc(y_out, 1)

            def finish_results(i, m):
                q = BP * i + m
                dve.wait_ge(y_full, Y_CREDIT + PAIRS + q + 1)
                for s in range(2):
                    dve.tensor_tensor(ys[:, 2 * m + s, :], O[m % 2][:, s * D:(s + 1) * D], scale_b[:, :], ALU.mult
                                      ).then_inc(y_read, 1)
                if m == 0:
                    dve.wait_ge(x_exp_in, 16 * (i + 1))
                if m % 2 == 0:
                    dve.wait_ge(ids_taken, taken(1, 2 * i + m // 2 + 1))
                for s in range(2):
                    dve.wait_ge(y_read, 2 * (Y_CREDIT + q) + s + 1)
                    x_e = x_exp[:, bass.ds(2 * q + s, 1), :].rearrange("p a d -> p (a d)")
                    dve.scalar_tensor_tensor(out=x_e, in0=ys[:, 2 * m + s, :], scalar=hw[:, bass.ds(2 * q + s, 1)],
                                             in1=x_e, op0=ALU.mult, op1=ALU.add).then_inc(y_final, 1)

            def expert_turn(L, i, first=False, last=False):
                for m in range(BP):
                    q = BP * i + m
                    if not (last and m == BP - 1):
                        low_rows(L, q + 1, (m + 1) % 2)
                    if m % 2 == 0 and L == 0 and not first:
                        dve.wait_ge(returned[m // 2], 16 * CHUNK * i)
                    if L == 0:
                        scale_results(q, m)
                    else:
                        finish_results(i, m)
                    for e, b, k in new_masks(L, i, m, last):
                        build_weight(e, k)

            def experts(L):
                low_rows(L, 0, 0)
                expert_turn(L, 0, first=True)
                with dve.Fori(1, E // BODY - 1) as i:
                    expert_turn(L, i)
                expert_turn(L, E // BODY - 1, last=True)

            def add_ffn(g):
                dve.wait_ge(loaded[g], 16)
                dve.wait_ge(half_done, 1)
                for j in range(J):
                    t = g * J + j
                    dve.scalar_tensor_tensor(out=xt[:, t, :], in0=xf[:, t, 0:D], scalar=half_w[:, t:t + 1],
                                             in1=xt[:, t, :], op0=ALU.mult, op1=ALU.add).then_inc(x1_done, 1)

            def add_and_norm_mem(g):
                add_ffn(g)
                dve.wait_ge(x1_done, J * (g + 1))
                norm_stats("A", g, 2 * GROUPS + g, g)

            def low_mem(g):
                for h in range(2):
                    c = slice(h * 2 * P, (h + 1) * 2 * P)
                    dve.wait_ge(xt_out, XT_ATT[g] + h + 1)
                    dve.tensor_tensor(xa_lo[:, g % 2, :, c].rearrange("p k (j c) -> p k j c", j=2),
                                      XT[h][:, :].rearrange("p (j k c) -> p k j c", j=2, k=KC),
                                      xa_hi[:, g % 2, :, c].rearrange("p k (j c) -> p k j c", j=2),
                                      ALU.subtract).then_inc(xt_lo, 1)

            def memory(g, c):
                n = KC * g + c
                dve.wait_ge(tg_done, n + 1)
                dve.wait_ge(pv_ready, n + 1)
                dve.scalar_tensor_tensor(out=store[:, c, :], in0=tanh_g[:, c, :], scalar=1.0,
                                         in1=PJ[1][:, 0:GT], op0=ALU.add, op1=ALU.mult).then_inc(st_done, 1)
                dve.wait_ge(st_done, n + 1)
                for h in range(SEQS):
                    s = slice(h * S, (h + 1) * S)
                    dve.tensor_tensor_scan(mem[:, c, s], decay[:, :], store[:, c, s], 0.0, ALU.mult,
                                           ALU.add).then_inc(mem_done, 1)
                dve.wait_ge(tq_done, n + 1)
                dve.wait_ge(mem_done, SEQS * (n + 1))
                if g > 0:
                    dve.wait_ge(ld_lo_done, KC * g)
                dve.scalar_tensor_tensor(out=load[:, c, :], in0=tanh_q[:, c, :], scalar=1.0, in1=mem[:, c, :],
                                         op0=ALU.add, op1=ALU.mult).then_inc(ld_done, 1)

            def add_mem_and_norm(g):
                for h in range(2):
                    t = slice(g * J + 2 * h, g * J + 2 * h + 2)
                    dve.wait_ge(o_ready, 2 * g + h + 1)
                    dve.tensor_tensor(xt[:, t, :], xt[:, t, :], O[h][:, :].rearrange("p (j d) -> p j d", j=2),
                                      ALU.add).then_inc(x2_done, 1)
                dve.wait_ge(x2_done, 2 * (g + 1))
                norm_stats("F", GROUPS + g, GROUPS + g, g)

            dve.memset(ones[:, :], 1.0).then_inc(ones_done, 1)
            dve.memset(decay[:, :], DECAY).then_inc(consts_done, 1)
            dve.wait_ge(iota_done, 1)
            dve.tensor_copy(expert[:, :], iota_e[:, :]).then_inc(consts_done, 1)
            dve.tensor_scalar(prefer[:, :], iota_e[:, :], -1.0, float(E), ALU.mult, ALU.add).then_inc(consts_done, 1)
            dve.sem_inc(w_ready, W_CREDIT)
            dve.sem_inc(y_out, Y_CREDIT)
            dve.sem_inc(y_read, 2 * Y_CREDIT)

            for g in range(GROUPS):
                dve.wait_ge(x_in[g], 16)
                norm_stats("F", g, g, g)
                if g == 1:
                    dve.wait_ge(small_T, 1)
                    dve.tensor_copy(rT[:, :, :], PJ[0][:, 0:KC * E].rearrange("p (k e) -> p k e", k=KC)
                                    ).then_inc(small_ready, 1)
                if g > 0:
                    norm_bias("F", g - 1, g - 1)
            dve.wait_ge(w_in, 16)
            dve.tensor_scalar(w_low, w_nat, -THRESH / 2, None, ALU.is_lt).then_inc(low_done, 1)
            norm_bias("F", GROUPS - 1, GROUPS - 1)
            dve.wait_ge(low_done, 1)
            dve.scalar_tensor_tensor(out=w_low, in0=w_nat, scalar=THRESH / 2, in1=w_low, op0=ALU.is_gt,
                                     op1=ALU.subtract).then_inc(quant_done, 1)
            dve.wait_ge(consts_done, 3)
            for g in range(GROUPS):
                choose(0, g)
                if g == 1:
                    dve.wait_ge(qT_full, 1)
                    dve.tensor_copy(w_qT[:, :, :], PJ[0][:, :].rearrange("p (k o) -> p k o", k=KC)).then_inc(qT_ready, 1)
                    dve.wait_ge(small_T, 2)
                    dve.tensor_scalar(half_b[:, :], PJ[1][:, 0:4], 0.5, None, ALU.mult).then_inc(small_ready, 1)
                number(0, g)
            for e in range(AHEAD):
                build_weight(e, e % 2)
            too_many(0)
            dve.wait_ge(att_in, 64)
            dve.tensor_scalar(w_raw[:, 3], w_raw[:, 3], GATE, None, ALU.mult).then_inc(wo_scaled, 1)
            dve.wait_ge(scale_in, 16)
            dve.wait_ge(mask_tested, M_CREDIT + AHEAD)
            experts(0)
            masks_have_low_bits()
            set_flag(0)
            top_weights(0, slice(0, TILES), half_w[:, :])
            dve.wait_ge(w_hi_done, 1)
            dve.tensor_tensor(w_lo[:, :, :, :], w_raw, w_hi[:, :, :, :], ALU.subtract).then_inc(w_lo_done, 1)
            rounds(0)

            add_and_norm_mem(0)
            add_ffn(1)
            norm_bias("A", 0, 2 * GROUPS)
            dve.wait_ge(x1_done, 2 * J)
            norm_stats("A", 1, 2 * GROUPS + 1, 1)
            low_mem(0)
            norm_bias("A", 1, 2 * GROUPS + 1)
            for i in range(GROUPS + 3):
                if i + 2 < GROUPS:
                    add_and_norm_mem(i + 2)
                if i < GROUPS:
                    memory(i, 0)
                if i + 1 < GROUPS:
                    low_mem(i + 1)
                if i == 3:
                    number(1, 0)
                    top_weights_group(0)
                if i + 2 < GROUPS:
                    norm_bias("A", i + 2, 2 * GROUPS + i + 2)
                if i < GROUPS:
                    memory(i, 1)
                if 0 <= i - 1 < GROUPS:
                    add_mem_and_norm(i - 1)
                if i > 3:
                    number(1, i - 3)
                    top_weights_group(i - 3)
                if 0 <= i - 1 < GROUPS:
                    norm_bias("F", GROUPS + i - 1, GROUPS + i - 1)
                if 0 <= i - 2 < GROUPS:
                    choose(1, i - 2)
            too_many(1)
            set_flag(1)
            rounds(1)
            experts(1)

        @block.tensor
        def _(pe):
            def transpose_group(kind, n, u, src):
                for h in range(2):
                    if u + h > 1:
                        pe.wait_ge(xt_out, u + h - 1)
                        if lo_before(u + h - 1) > 0:
                            pe.wait_ge(xt_lo, lo_before(u + h - 1))
                    for j in range(2):
                        pe.wait_ge(ln[kind]["xn"], J * n + 2 * h + j + 1)
                        for k in range(KC):
                            at = (j * KC + k) * P
                            ins = pe.transpose(XT[h][:, at:at + P], src[:, 2 * h + j, k * P:(k + 1) * P], ident[:, :])
                    ins.then_inc(xt_full, 1)

            def transpose_mem(g):
                transpose_group("A", g, XT_ATT[g], xa)

            def transpose_ffn(L, g):
                transpose_group("F", L * GROUPS + g, XT_FFN[L][g], xf[:, tiles(g), 0:D])

            def logits(L, g):
                n = L * GROUPS + g
                if L == 0 and g > 1:
                    pe.wait_ge(lg_read, (J + 1) * (n - 1))
                if L == 1 and g < 2:
                    pe.wait_ge(lg_read, (J + 1) * n)
                    pe.wait_ge(low_f_done, 1)
                    pe.wait_ge(pos_done, n)
                if L == 1 and g >= 2:
                    pe.wait_ge(tg_done, KC * GROUPS)
                if L == 1 and g == 3:
                    pe.wait_ge(lg_read, (J + 1) * n)
                for j in range(J):
                    pe.wait_ge(xt_out, XT_FFN[L][g] + j // 2 + 1)
                    for k in range(KC):
                        ins = pe.matmul(LG[L][g][:, j * E:(j + 1) * E], xfT[:, k, j * P:(j + 1) * P], rT[:, k, :],
                                        start=(k == 0), stop=(k == KC - 1))
                ins.then_inc(lg_ready, 1)

            def ranks_before(L, g):
                n = L * GROUPS + g
                if n > 0:
                    pe.wait_ge(pos_done, n)
                if L == 1 and g < 1:
                    pe.wait_ge(lg_read, (J + 1) * (n + 1))
                if L == 1 and g >= 1:
                    pe.wait_ge(tq_done, KC * GROUPS)
                if g > 0:
                    pe.wait_ge(hot_done, n)
                rk = RK[L][g].rearrange("p (j e) -> p j e", j=J)
                pe.matmul(rk, ones[:, :], expert[:, :].unsqueeze(1).to_broadcast([P, J, E]), start=True, stop=False)
                for t in range(g * J):
                    pe.matmul(rk, ones[:, :], hot[:, t:t + 1, :].to_broadcast([P, J, E]), start=False, stop=False)

            def ranks(L, g):
                n = L * GROUPS + g
                pe.wait_ge(hot_done, n + 1)
                rk = RK[L][g].rearrange("p (j e) -> p j e", j=J)
                for j in range(J - 1):
                    pe.matmul(rk[:, j + 1:J, :], ones[:, :],
                              hot[:, g * J + j:g * J + j + 1, :].to_broadcast([P, J - 1 - j, E]), start=False, stop=False)
                pe.matmul(rk, below[:, :], hot[:, tiles(g), :], start=False, stop=True).then_inc(rk_ready, 1)

            def counts(L):
                pe.wait_ge(lg_read, (J + 1) * GROUPS * (L + 1))
                pe.wait_ge(pos_done, GROUPS * (L + 1))
                for t in range(TILES):
                    ins = pe.matmul(CN, ones[:, :], hot[:, t, :], start=(t == 0), stop=(t == TILES - 1))
                ins.then_inc(cn_ready, 1)

            def mask_transposes(e, b, masks, m):
                pe.wait_ge(w_ready, e - 1 + W_CREDIT)
                for c in range(KC):
                    for k in range(KC):
                        at = k * D + c * P
                        ins = pe.transpose(PJ[b][:, at:at + P],
                                           masks[:, KC * m + c, k * P:(k + 1) * P],
                                           ident[:, :])
                ins.then_inc(mask_T, 1)

            def rows_transposes(L, q, m):
                b = m % 2
                if isinstance(q, int) and q < 2:
                    pe.wait_ge(xt_out, XT_EXP[L] + q - 1)
                    if lo_before(XT_EXP[L] + q - 1) > 0:
                        pe.wait_ge(xt_lo, lo_before(XT_EXP[L] + q - 1))
                else:
                    pe.wait_ge(xt_lo, LO_EXP[L] + q - 1)
                for s in range(2):
                    for k in range(KC):
                        at = (s * KC + k) * P
                        ins = pe.transpose(XT[b][:, at:at + P], xs[:, 2 * m + s, k * P:(k + 1) * P], ident[:, :])
                ins.then_inc(xt_full, 1)

            def product(L, q, m):
                b = m % 2
                pe.wait_ge(xt_lo, LO_EXP[L] + q + 1)
                if L == 0:
                    pe.wait_ge(w_ready, W_CREDIT + 2 * q + 2)
                    pe.wait_ge(y_out, Y_CREDIT + q - 1)
                else:
                    pe.wait_ge(y_read, 2 * (Y_CREDIT + q - 1))
                for s in range(2):
                    for k in range(KC):
                        for n, part in enumerate((xs_hi, xs_lo)):
                            ins = pe.matmul(O[b][:, s * D:(s + 1) * D], part[:, b, (s * KC + k) * P:(s * KC + k + 1) * P],
                                            w_exp[:, bass.ds(2 * q + s, 1), k, :].rearrange("p a o -> p (a o)"),
                                            start=(k == 0 and n == 0), stop=(k == KC - 1 and n == 1))
                ins.then_inc(y_full, 1)

            def expert_turn(L, i, last=False):
                for m in range(BP):
                    q = BP * i + m
                    if m == 1:
                        pe.wait_ge(xs_in[1], 16 * (CHUNKS // 2 * L + i + 1))
                    if m == BP - 1 and not last:
                        pe.wait_ge(xs_in[0], 16 * (CHUNKS // 2 * L + i + 2))
                    if not (last and m == BP - 1):
                        rows_transposes(L, q + 1, (m + 1) % BP)
                    product(L, q, m)
                    for e, b, k in new_masks(L, i, m, last):
                        if k == 0:
                            pe.wait_ge(mask_in[b], 16 * (i + 2))
                        mask_transposes(e, k, mask_raw[:, b], k)

            def experts(L):
                pe.wait_ge(xs_in[0], 16 * (CHUNKS // 2 * L + 1))
                rows_transposes(L, 0, 0)
                with pe.Fori(0, E // BODY - 1) as i:
                    expert_turn(L, i)
                expert_turn(L, E // BODY - 1, last=True)

            def rounds(L):
                with pe.If(rounds_needed(pe, L)):
                    v = rd[L]
                    if L == 0:
                        pe.wait_ge(y_out, PAIRS + Y_CREDIT)
                    else:
                        pe.wait_ge(x2_done, 2 * GROUPS)
                        pe.wait_ge(xt_out, XT_EXP[1])
                    with pe.Fori(0, ROUNDS * E) as n:
                        pe.wait_ge(v["rows"], 16 * (L + 1) * (n + 1))
                        for k in range(KC):
                            pe.transpose(XT[0][:, k * P:(k + 1) * P], xs[:, 0, k * P:(k + 1) * P], ident[:, :])
                        pe.wait_ge(v["mask"], 16 * (n + 1))
                        for c in range(KC):
                            for k in range(KC):
                                at = k * D + c * P
                                ins = pe.transpose(PJ[0][:, at:at + P], mask_raw[:, 0, c, k * P:(k + 1) * P], ident[:, :])
                        ins.then_inc(v["T"], 1)
                        pe.wait_ge(v["xT"], n + 1)
                        pe.wait_ge(v["w"], n + 1)
                        for k in range(KC):
                            ins = pe.matmul(O[0][:, 0:D], xs_one[:, k, :], w_one[:, k, :],
                                            start=(k == 0), stop=(k == KC - 1))
                        ins.then_inc(v["y"], 1)
                    pe.wait_ge(v["yout"], ROUNDS * E)

            def project(g, c):
                pe.wait_ge(xt_out, XT_ATT[g] + 2)
                n = KC * g + c
                m = slice(c * P, (c + 1) * P)
                for w, ready, free in ((0, pg_ready, tg_done), (1, pv_ready, st_done), (2, pq_ready, tq_done)):
                    if n > 0:
                        pe.wait_ge(free, n)
                    for a, (wx, xx) in enumerate(((w_hi, xa_hi), (w_lo, xa_hi), (w_hi, xa_lo))):
                        if w == 0 and a == 2:
                            pe.wait_ge(xt_lo, lo_before(XT_ATT[g] + 2))
                        for k in range(KC):
                            ins = pe.matmul(PJ[w][:, 0:GT], wx[:, w, k, m], xx[:, g % 2, k, :],
                                            start=(k == 0 and a == 0), stop=(k == KC - 1 and a == 2))
                    ins.then_inc(ready, 1)

            def out_project(g):
                pe.wait_ge(ld_lo_done, KC * (g + 1))
                for h in range(2):
                    if g > 0:
                        pe.wait_ge(x2_done, 2 * g)
                    for j in range(2):
                        t = slice((2 * h + j) * P, (2 * h + j + 1) * P)
                        for c in range(KC):
                            for a, (lx, wx) in enumerate(((load_hi, w_hi), (load_hi, w_lo), (load_lo, w_hi))):
                                ins = pe.matmul(O[h][:, j * D:(j + 1) * D], lx[:, c, t], wx[:, 3, c, :],
                                                start=(c == 0 and a == 0), stop=(c == KC - 1 and a == 2))
                    ins.then_inc(o_ready, 1)

            pe.sem_inc(y_full, Y_CREDIT)
            pe.wait_ge(ident_done, 1)
            pe.wait_ge(r_in, 16)
            for k in range(KC):
                ins = pe.transpose(PJ[0][:, k * E:(k + 1) * E], r_nat[:, k * P:(k + 1) * P], ident[0:E, 0:E])
            ins.then_inc(small_T, 1)

            def chunk_transposes(c):
                pe.wait_ge(mask_in[c], 16)
                for m in range(CHUNK):
                    mask_transposes(CHUNK * c + m, m % 2, early_masks[c], m)

            transpose_ffn(0, 0)
            pe.wait_ge(small_ready, 1)
            logits(0, 0)
            transpose_ffn(0, 1)
            pe.wait_ge(below_done, 1)
            pe.wait_ge(consts_done, 3)
            for g in range(GROUPS):
                ranks_before(0, g)
                ranks(0, g)
                if g + 1 < GROUPS:
                    logits(0, g + 1)
                if g + 2 < GROUPS:
                    transpose_ffn(0, g + 2)
                if g == 0:
                    pe.wait_ge(quant_done, 1)
                    for c in range(KC):
                        for k in range(KC):
                            ins = pe.transpose(PJ[0][:, k * D + c * P:k * D + (c + 1) * P], w_low[:, c, k * P:(k + 1) * P],
                                               ident[:, :])
                    ins.then_inc(qT_full, 1)
                    pe.wait_ge(b_in, 32)
                    pe.transpose(PJ[1][:, 0:4], vec_rows[:, :], ident[0:4, 0:4]).then_inc(small_T, 1)
            pe.wait_ge(small_ready, 2)
            pe.wait_ge(qT_ready, 1)
            chunk_transposes(0)
            counts(0)
            for c in range(1, AHEAD // CHUNK):
                chunk_transposes(c)
            experts(0)
            pe.wait_ge(lowmax_done, 1)
            pe.wait_ge(most_done, 1)
            pe.matmul(LOW, ones_f[:, 0:P], low_max[:, :], start=True, stop=True).then_inc(low_ready, 1)
            rounds(0)

            pe.wait_ge(w_lo_done, 1)
            pe.wait_ge(y_out, PAIRS + Y_CREDIT)
            transpose_mem(0)
            for i in range(GROUPS + 2):
                if i < GROUPS:
                    project(i, 0)
                if i + 1 < GROUPS:
                    transpose_mem(i + 1)
                if i == 3:
                    ranks_before(1, 0)
                    ranks(1, 0)
                if i < GROUPS:
                    project(i, 1)
                if 0 <= i - 1 < GROUPS:
                    out_project(i - 1)
                if i >= GROUPS:
                    ranks_before(1, i - 3)
                    ranks(1, i - 3)
                if i >= 2:
                    transpose_ffn(1, i - 2)
                    logits(1, i - 2)
            ranks_before(1, GROUPS - 1)
            ranks(1, GROUPS - 1)
            counts(1)
            pe.wait_ge(x2_done, 2 * GROUPS)
            rounds(1)
            experts(1)


_INS = ["L0_attn_x", "L0_attn_Wv", "L0_attn_Wg", "L0_attn_bg", "L0_attn_Wq", "L0_attn_bq", "L0_attn_Wo",
        "L0_ffn_weight", "L0_ffn_scale", "L0_ffn_expert_masks", "L0_ffn_router_w"]


def kernel(**inputs):
    import concourse.bacc as bacc
    from concourse.bass_utils import run_bass_kernel_spmd

    nc = bacc.Bacc("TRN2", target_bir_lowering=False, num_devices=1)
    arrays, args = {}, []
    for name in _INS:
        a = np.ascontiguousarray(inputs[name])
        arrays[f"in_{name}"] = a
        args.append(nc.dram_tensor(f"in_{name}", a.shape, mybir.dt.from_np(a.dtype), kind="ExternalInput").ap())
    x = arrays["in_L0_attn_x"]
    out = nc.dram_tensor("out_x", x.shape, F32, kind="ExternalOutput").ap()
    macaron_block(nc, *args, out)
    r = run_bass_kernel_spmd(nc, [arrays], core_ids=[0])
    return r.results[0]["out_x"]
```
